# Optimizing a Trainium2 kernel written in Bass

```python
import numpy as np
import jax
import jax.numpy as jnp

def _softmax(x, axis=-1):
    return jax.nn.softmax(x, axis=axis)

def _gelu(x):
    return jax.nn.gelu(x, approximate=True)

def _silu(x):
    return jax.nn.silu(x)

def _sigmoid(x):
    return jax.nn.sigmoid(x)

def _layernorm(x, axis=-1, eps=1e-05):
    m = jnp.mean(x, axis=axis, keepdims=True)
    v = jnp.var(x, axis=axis, keepdims=True)
    return (x - m) / jnp.sqrt(v + eps)

def _scatter_add(tgt, idx, src, axis=0):
    return tgt.at[idx].add(src)

def _segment_sum(src, seg, n):
    return jax.ops.segment_sum(src, seg, n)
kernel_name = 'mk_seq_preln_d1_jaxref_r4_ec1551'

def setup_inputs(seed: int=0):
    np.random.seed(seed)
    _w = jnp.asarray

    def _L0_attn_setup():
        import jax, jax.numpy as jnp
        import numpy as np
        B, T, D = (4, 1024, 256)
        NEG_CLAMP = -30.0
        EPS = 1e-09

        def _wkv_scan(k, v, w, u):
            Bn, Tn, Dn = k.shape
            p0 = jnp.full((Bn, Dn), -jnp.inf, k.dtype)
            q0 = jnp.zeros((Bn, Dn), k.dtype)

            def step(carry, kv_t):
                p, q = carry
                k_t, v_t = kv_t
                new_p = jnp.maximum(p, u + k_t)
                scale_old = jnp.exp(jnp.maximum(p - new_p, NEG_CLAMP))
                scale_cur = jnp.exp(jnp.maximum(u + k_t - new_p, NEG_CLAMP))
                wkv_t = (scale_old * q + scale_cur * v_t) / (scale_old + scale_cur + EPS)
                new_p2 = jnp.maximum(p + w, k_t)
                scale_prev = jnp.exp(jnp.maximum(p + w - new_p2, NEG_CLAMP))
                scale_new = jnp.exp(jnp.maximum(k_t - new_p2, NEG_CLAMP))
                q2 = scale_prev * q + scale_new * v_t
                return ((new_p2, q2), wkv_t)
            kT = jnp.swapaxes(k, 0, 1)
            vT = jnp.swapaxes(v, 0, 1)
            _, wkvT = jax.lax.scan(step, (p0, q0), (kT, vT))
            return jnp.swapaxes(wkvT, 0, 1)
        key = jax.random.key(seed)
        ks = jax.random.split(key, 10)
        s = 0.02
        return {'x': jax.random.normal(ks[0], (B, T, D), jnp.float32), 'time_mix_k': jax.random.uniform(ks[1], (D,), jnp.float32), 'time_mix_v': jax.random.uniform(ks[2], (D,), jnp.float32), 'time_mix_r': jax.random.uniform(ks[3], (D,), jnp.float32), 'W_k': jax.random.normal(ks[4], (D, D), jnp.float32) * s, 'W_v': jax.random.normal(ks[5], (D, D), jnp.float32) * s, 'W_r': jax.random.normal(ks[6], (D, D), jnp.float32) * s, 'W_o': jax.random.normal(ks[7], (D, D), jnp.float32) * s, 'time_decay': -(1.0 + jax.random.uniform(ks[8], (D,), jnp.float32)), 'time_first': 0.1 * jax.random.normal(ks[9], (D,), jnp.float32)}
    _L0_attn_in = _L0_attn_setup()

    def _L0_ffn_setup():
        import jax, jax.numpy as jnp
        import numpy as np
        D_IN, D_HID = (256, 1024)

        def _ternary(key, shape):
            return jax.random.randint(key, shape, -1, 2).astype(jnp.float32)

        def _tlin(x, w, s):
            return jnp.einsum('bsi,oi->bso', x, w) * s
        key = jax.random.key(seed)
        ks = jax.random.split(key, 12)
        inv = lambda fan: 1.0 / np.sqrt(fan).astype(np.float32)
        return {'x': jax.random.normal(ks[0], (4, 512, D_IN), dtype=jnp.float32), 'w1_w': _ternary(ks[1], (D_HID, D_IN)), 'w1_s': jax.random.uniform(ks[2], (D_HID,), dtype=jnp.float32) * inv(D_IN), 'w2_w': _ternary(ks[3], (D_HID, D_IN)), 'w2_s': jax.random.uniform(ks[4], (D_HID,), dtype=jnp.float32) * inv(D_IN), 'h1_w': _ternary(ks[5], (D_HID, D_HID)), 'h1_s': jax.random.uniform(ks[6], (D_HID,), dtype=jnp.float32) * inv(D_HID), 'h2_w': _ternary(ks[7], (D_HID, D_HID)), 'h2_s': jax.random.uniform(ks[8], (D_HID,), dtype=jnp.float32) * inv(D_HID), 'w3_w': _ternary(ks[9], (D_IN, D_HID)), 'w3_s': jax.random.uniform(ks[10], (D_IN,), dtype=jnp.float32) * inv(D_HID)}
    _L0_ffn_in = _L0_ffn_setup()
    _d = {'L0_attn_x': _L0_attn_in['x'], 'L0_attn_time_mix_k': _L0_attn_in['time_mix_k'], 'L0_attn_time_mix_v': _L0_attn_in['time_mix_v'], 'L0_attn_time_mix_r': _L0_attn_in['time_mix_r'], 'L0_attn_W_k': _L0_attn_in['W_k'], 'L0_attn_W_v': _L0_attn_in['W_v'], 'L0_attn_W_r': _L0_attn_in['W_r'], 'L0_attn_W_o': _L0_attn_in['W_o'], 'L0_attn_time_decay': _L0_attn_in['time_decay'], 'L0_attn_time_first': _L0_attn_in['time_first'], 'L0_ffn_w1_w': _L0_ffn_in['w1_w'], 'L0_ffn_w1_s': _L0_ffn_in['w1_s'], 'L0_ffn_w2_w': _L0_ffn_in['w2_w'], 'L0_ffn_w2_s': _L0_ffn_in['w2_s'], 'L0_ffn_h1_w': _L0_ffn_in['h1_w'], 'L0_ffn_h1_s': _L0_ffn_in['h1_s'], 'L0_ffn_h2_w': _L0_ffn_in['h2_w'], 'L0_ffn_h2_s': _L0_ffn_in['h2_s'], 'L0_ffn_w3_w': _L0_ffn_in['w3_w'], 'L0_ffn_w3_s': _L0_ffn_in['w3_s']}
    _x0 = _d['L0_attn_x']
    _d['L0_attn_x'] = jax.random.normal(jax.random.fold_in(jax.random.key(seed), 1), (2, 4096, 256), dtype=_x0.dtype)
    del _x0
    return _d

def reference(L0_attn_x, L0_attn_time_mix_k, L0_attn_time_mix_v, L0_attn_time_mix_r, L0_attn_W_k, L0_attn_W_v, L0_attn_W_r, L0_attn_W_o, L0_attn_time_decay, L0_attn_time_first, L0_ffn_w1_w, L0_ffn_w1_s, L0_ffn_w2_w, L0_ffn_w2_s, L0_ffn_h1_w, L0_ffn_h1_s, L0_ffn_h2_w, L0_ffn_h2_s, L0_ffn_w3_w, L0_ffn_w3_s):

    def _L0_attn_ref(x, time_mix_k, time_mix_v, time_mix_r, W_k, W_v, W_r, W_o, time_decay, time_first):
        import jax, jax.numpy as jnp
        import numpy as np
        B, T, D = (4, 1024, 256)
        NEG_CLAMP = -30.0
        EPS = 1e-09

        def _wkv_scan(k, v, w, u):
            Bn, Tn, Dn = k.shape
            p0 = jnp.full((Bn, Dn), -jnp.inf, k.dtype)
            q0 = jnp.zeros((Bn, Dn), k.dtype)

            def step(carry, kv_t):
                p, q = carry
                k_t, v_t = kv_t
                new_p = jnp.maximum(p, u + k_t)
                scale_old = jnp.exp(jnp.maximum(p - new_p, NEG_CLAMP))
                scale_cur = jnp.exp(jnp.maximum(u + k_t - new_p, NEG_CLAMP))
                wkv_t = (scale_old * q + scale_cur * v_t) / (scale_old + scale_cur + EPS)
                new_p2 = jnp.maximum(p + w, k_t)
                scale_prev = jnp.exp(jnp.maximum(p + w - new_p2, NEG_CLAMP))
                scale_new = jnp.exp(jnp.maximum(k_t - new_p2, NEG_CLAMP))
                q2 = scale_prev * q + scale_new * v_t
                return ((new_p2, q2), wkv_t)
            kT = jnp.swapaxes(k, 0, 1)
            vT = jnp.swapaxes(v, 0, 1)
            _, wkvT = jax.lax.scan(step, (p0, q0), (kT, vT))
            return jnp.swapaxes(wkvT, 0, 1)
        x_prev = jnp.pad(x[:, :-1, :], ((0, 0), (1, 0), (0, 0)))
        xk = x * time_mix_k + x_prev * (1.0 - time_mix_k)
        xv = x * time_mix_v + x_prev * (1.0 - time_mix_v)
        xr = x * time_mix_r + x_prev * (1.0 - time_mix_r)
        k = jnp.einsum('btd,ed->bte', xk, W_k)
        v = jnp.einsum('btd,ed->bte', xv, W_v)
        r = jax.nn.sigmoid(jnp.einsum('btd,ed->bte', xr, W_r))
        wkv = _wkv_scan(k, v, time_decay, time_first)
        y = r * wkv
        return jnp.einsum('btd,ed->bte', y, W_o)

    def _L0_ffn_ref(x, w1_w, w1_s, w2_w, w2_s, h1_w, h1_s, h2_w, h2_s, w3_w, w3_s):
        import jax, jax.numpy as jnp
        import numpy as np
        D_IN, D_HID = (256, 1024)

        def _ternary(key, shape):
            return jax.random.randint(key, shape, -1, 2).astype(jnp.float32)

        def _tlin(x, w, s):
            return jnp.einsum('bsi,oi->bso', x, w) * s
        h = jax.nn.silu(_tlin(x, w1_w, w1_s)) * _tlin(x, w2_w, w2_s)
        h = jax.nn.gelu(_tlin(h, h1_w, h1_s), approximate=False)
        h = jax.nn.gelu(_tlin(h, h2_w, h2_s), approximate=False)
        return _tlin(h, w3_w, w3_s)
    x = L0_attn_x
    x = x + _L0_attn_ref(_layernorm(x, axis=-1), L0_attn_time_mix_k, L0_attn_time_mix_v, L0_attn_time_mix_r, L0_attn_W_k, L0_attn_W_v, L0_attn_W_r, L0_attn_W_o, L0_attn_time_decay, L0_attn_time_first)
    x = x + _L0_ffn_ref(_layernorm(x, axis=-1), L0_ffn_w1_w, L0_ffn_w1_s, L0_ffn_w2_w, L0_ffn_w2_s, L0_ffn_h1_w, L0_ffn_h1_s, L0_ffn_h2_w, L0_ffn_h2_s, L0_ffn_w3_w, L0_ffn_w3_s)
    return x

_drawn_inputs = setup_inputs


def setup_inputs(seed=0):
    import zlib

    import numpy as np

    out = dict(_drawn_inputs(seed))
    spreads = {}
    factors = {}
    for name, (base, spread) in spreads.items():
        noise = np.random.default_rng([zlib.crc32(name.encode()), seed]).standard_normal(out[name].shape)
        drawn = base * np.exp(spread * noise) if base else spread * noise
        out[name] = jnp.asarray(drawn.astype(out[name].dtype))
    for name, factor in factors.items():
        out[name] = (out[name] * factor).astype(out[name].dtype)
    return out
```

```python
from contextlib import ExitStack

import numpy as np

import concourse.bass as bass
from concourse import mybir

F32 = mybir.dt.float32
F32R = mybir.dt.float32r
I32 = mybir.dt.int32
ALU = mybir.AluOpType
ACT = mybir.ActivationFunctionType
AX_X = mybir.AxisListType.X

P = 128
LN_EPS = 1e-5
WKV_EPS = 1e-9
CLAMP = 30.0
LOWEST = float(np.finfo(np.float32).min)
RSQRT_SEED = 0x5F3759DF
NEWTON_STEPS = 3
LOW_BITS = 0xFFF


def stand_alone(eng, spare):
    eng.sem_inc(spare, 1)


class Tally:

    def __init__(self, ctx, nc, name, per, unit=1):
        self.sem = ctx.enter_context(nc.semaphore(name))
        self.per, self.unit = per, unit

    def start(self, eng):
        eng.sem_inc(self.sem, self.per * self.unit)

    def wait(self, eng, tile, k=None):
        k = self.per if k is None else k
        eng.wait_ge(self.sem, tile * (self.per * self.unit) + (self.per + k) * self.unit)

    def add(self, instruction):
        instruction.then_inc(self.sem, self.unit)
        return instruction


class Chain:

    def __init__(self, ctx, nc, name, eng, per):
        self.sem = ctx.enter_context(nc.semaphore(name))
        self.eng, self.per, self.n = eng, per, 0

    def link(self, instruction):
        instruction.then_inc(self.sem, 1)
        self.n += 1

    def wait(self, tile):
        self.eng.wait_ge(self.sem, tile * self.per + self.n)

    def done(self, instruction, tile):
        self.link(instruction)
        self.wait(tile)

    def end_tile(self):
        assert self.n == self.per, (self.n, self.per)
        self.n = 0


def build(nc, x, vectors, w_mix, w_ffn, s3, out):
    n_seq, T, D = x.shape
    DC = D // P
    H = 1024
    HC = H // P
    TILE = 512
    SEG = TILE // n_seq
    HALVES = SEG // P
    NB = TILE // P
    NT = T // SEG
    SW = DC * TILE
    W12, HH, W3 = DC * H, HC * H, HC * D
    assert vectors.shape[1] == 5 * DC + 4 * HC and w_ffn.shape[1] == 2 * W12 + 2 * HH + W3

    x_tiles = x.rearrange("n (i h p) d -> n i p h d", h=HALVES, p=P)
    out_tiles = out.rearrange("n (i h p) d -> n i p h d", h=HALVES, p=P)

    with ExitStack() as ctx:
        def sb(name, shape, dt=F32):
            return ctx.enter_context(nc.sbuf_tensor(name, shape, dt))

        def overlay(name, shape, dt):
            with nc.sbuf_tensor(name, shape, dt) as t:
                return t

        def tally(name, per, unit=1):
            return Tally(ctx, nc, name, per, unit)

        NW = 2 * W12 + 2 * HH + W3
        w_raw = overlay("w_raw", [P, NW], F32)
        w_rnd = sb("w_rnd", [P, NW], F32R)
        wm = sb("wm", [P, 4, DC, D])
        x_in = sb("x_in", [P, NB, D])
        norm = sb("norm", [P, NB * D])
        seq = sb("seq", [P, DC, n_seq, SEG + 1])
        mix_k = sb("mix_k", [P, DC, TILE])
        mix_v = sb("mix_v", [P, DC, TILE])
        mix_r = sb("mix_r", [P, DC, TILE])
        x2_hi = overlay("x2_hi", [P, DC, TILE], F32R)
        k_sb = sb("k_sb", [P, DC, TILE])
        x2_lo = overlay("x2_lo", [P, DC, TILE], F32R)
        r_sb = sb("r_sb", [P, DC, TILE])
        v_sb = sb("v_sb", [P, DC, TILE])
        x1_next = sb("x1_next", [P, NB, D])
        x1 = sb("x1", [P, NB, D])
        check = overlay("check", [P, 2 * W12 // 2], I32)
        ha_hi = sb("ha_hi", [P, HC, TILE], F32R)
        ha_lo = sb("ha_lo", [P, HC, TILE], F32R)
        hb_hi = sb("hb_hi", [P, HC, TILE], F32R)
        hb_lo = sb("hb_lo", [P, HC, TILE], F32R)
        vec = sb("vec", [P, vectors.shape[1]])
        s3_row = sb("s3_row", [P, D])
        ident = sb("ident", [P, P])
        carry_x = sb("carry_x", [P, DC, n_seq, 1])
        carry_p = sb("carry_p", [P, DC, n_seq, 1])
        carry_q = sb("carry_q", [P, DC, n_seq, 1])
        stats = sb("stats", [P, NB, 6])
        moments = sb("moments", [P, NB, 2])
        var = sb("var", [P, NB])
        shifted = sb("shifted", [P, NB], I32)
        rstd = sb("rstd", [P, NB])
        newton = sb("newton", [P, 2, NB])
        inexact = sb("inexact", [P, 1])
        ones = sb("ones", [P, 1])
        general = sb("general", [1, 1], I32)

        F = [ctx.enter_context(nc.psum_tensor(f"ffn{i}", [P, 512], F32)) for i in range(4)]
        A = [ctx.enter_context(nc.psum_tensor(f"att{i}", [P, 512], F32)) for i in range(4)]
        PAIRS = [(F[2], F[3]), (F[0], F[1]), (A[0], A[1]), (A[2], A[3])]
        KVR_BANK = [A[2], A[3], A[0], A[1], A[2], A[3]]

        tmk, tmv, tmr, decay, first = (vec[:, DC * j:DC * (j + 1)] for j in range(5))
        s1, s2, sh1, sh2 = (vec[:, 5 * DC + HC * j:5 * DC + HC * (j + 1)] for j in range(4))
        norm_tok = norm[:].rearrange("p (b d) -> p b d", b=NB)
        norm_ch = norm[:].rearrange("p (c t) -> p c t", c=DC)
        out_tok = mix_v[:].rearrange("p c t -> p (c t)").rearrange("p (b d) -> p b d", b=NB)

        def by_seq(ap):
            return ap.rearrange("p c (n t) -> p c n t", n=n_seq)

        now, before = seq[:, :, :, 1:], seq[:, :, :, 0:SEG]

        def ffn_weights(w):
            a = 0
            parts = []
            for n, c in ((W12, DC), (W12, DC), (HH, HC), (HH, HC), (W3, HC)):
                parts.append(w[:, a:a + n].rearrange("p (c o) -> p c o", c=c))
                a += n
            return parts

        ld_const = ctx.enter_context(nc.semaphore("ld_const"))
        ld_w = ctx.enter_context(nc.semaphore("ld_w"))
        setup_pool = ctx.enter_context(nc.semaphore("setup_pool"))
        setup_dve = ctx.enter_context(nc.semaphore("setup_dve"))
        setup_ident = ctx.enter_context(nc.semaphore("setup_ident"))
        spare = ctx.enter_context(nc.semaphore("spare"))
        flag_sum = ctx.enter_context(nc.semaphore("flag_sum"))
        flag_set = ctx.enter_context(nc.semaphore("flag_set"))
        rounded = ctx.enter_context(nc.semaphore("rounded"))
        rounded_dve = ctx.enter_context(nc.semaphore("rounded_dve"))
        ld_x = tally("ld_x", n_seq, 16)
        st_out = tally("st_out", n_seq, 16)
        pe_xT, pe_kvr, pe_wo, pe_x2T = (tally(n, k) for n, k in (("pe_xT", DC), ("pe_kvr", 3 * DC), ("pe_wo", 2), ("pe_x2T", DC)))
        pe_ab, pe_h1, pe_h2, pe_w3 = (tally(n, k) for n, k in (("pe_ab", 2 * HC), ("pe_h1", HC), ("pe_h2", HC), ("pe_w3", 2)))
        act_x, act_kvr, act_exp, act_x2 = (tally(n, k) for n, k in (("act_x", 4), ("act_kvr", 3 * DC), ("act_exp", 5), ("act_x2", DC)))
        act_silu, act_hi, act_hi1, act_h1, act_hi2, act_h2 = (tally(n, HC) for n in ("act_silu", "act_hi", "act_hi1", "act_h1", "act_hi2", "act_h2"))
        dve_seed1, dve_seed2, dve_norm1, dve_norm2 = (tally(n, k) for n, k in (("dve_seed1", 1), ("dve_seed2", 1), ("dve_norm1", NB), ("dve_norm2", NB)))
        dve_mix, dve_pre, dve_q, dve_y, dve_x1, dve_x2 = (tally(n, k) for n, k in (
            ("dve_mix", 3 * DC), ("dve_pre", 4), ("dve_q", 1), ("dve_y", 1), ("dve_x1", 2), ("dve_x2", DC)))
        dve_prod, dve_lo, dve_lo1, dve_lo2, dve_fin = (tally(n, k) for n, k in (
            ("dve_prod", HC), ("dve_lo", HC), ("dve_lo1", HC), ("dve_lo2", HC), ("dve_fin", 2)))
        pool_rs1, pool_rs2, pool_num, pool_out, pool_x1 = (tally(n, k) for n, k in (
            ("pool_rs1", 1), ("pool_rs2", 1), ("pool_num", 1), ("pool_out", 2), ("pool_x1", 1)))

        block = ctx.enter_context(nc.Block())

        @block.sync
        def _(sp):
            for t in (ld_x, st_out):
                t.start(sp)

            def load_x(t):
                dve_x1.wait(sp, t - 1)
                for n in range(n_seq):
                    ld_x.add(sp.dma_start(x_in[:, HALVES * n:HALVES * (n + 1), :], x_tiles[n, t]))

            def store(i):
                for j in range(2):
                    pool_out.wait(sp, i, j + 1)
                    st_out.add(sp.dma_start(out_tiles[j, i], out_tok[:, HALVES * j:HALVES * (j + 1), :]))

            load_x(0)
            sp.dma_start(vec[:], vectors).then_inc(ld_const, 16)
            sp.dma_start(wm[:], w_mix).then_inc(ld_const, 16)
            sp.dma_start(s3_row[:], s3.broadcast_to([P, D])).then_inc(ld_const, 16)
            a = 0
            for n in (W12, W12, HH, HH, W3):
                sp.dma_start(w_raw[:, a:a + n], w_ffn[:, a:a + n]).then_inc(ld_w, 16)
                a += n
            with sp.Fori(0, NT - 1) as i:
                load_x(i + 1)
                store(i)
            store(NT - 1)
            st_out.wait(sp, NT - 1)

        @block.tensor
        def _(pe):
            for t in (pe_xT, pe_kvr, pe_wo, pe_x2T, pe_ab, pe_h1, pe_h2, pe_w3):
                t.start(pe)

            def transpose_x(t):
                dve_norm1.wait(pe, t)
                for c in range(DC):
                    for b in range(NB):
                        mm = pe.transpose(A[c][:, b * P:(b + 1) * P], norm_tok[:, b, c * P:(c + 1) * P], ident[:])
                    pe_xT.add(mm)

            def project(t):
                for j in range(3 * DC):
                    which, e = divmod(j, DC)
                    src = (mix_k, mix_v, mix_r)[which]
                    dve_mix.wait(pe, t, j // DC * DC + DC)
                    if j >= 4:
                        act_kvr.wait(pe, t, j - 3)
                    for c in range(DC):
                        mm = pe.matmul(KVR_BANK[j][:], wm[:, which, c, e * P:(e + 1) * P], src[:, c, :],
                                       start=(c == 0), stop=(c == DC - 1))
                    pe_kvr.add(mm)

            def project_out(t):
                dve_y.wait(pe, t)
                for b in range(NB):
                    for c in range(DC):
                        mm = pe.matmul(A[b // 2][:, (b % 2) * D:(b % 2 + 1) * D], v_sb[:, c, b * P:(b + 1) * P],
                                       wm[:, 3, c, :], start=(c == 0), stop=(c == DC - 1))
                    if b % 2:
                        pe_wo.add(mm)

            def transpose_x2(t):
                dve_norm2.wait(pe, t)
                for c in range(DC):
                    for b in range(NB):
                        mm = pe.transpose(A[2 + c][:, b * P:(b + 1) * P], norm_tok[:, b, c * P:(c + 1) * P], ident[:])
                    pe_x2T.add(mm)

            def mlp(exact):
                w1, w2, wh1, wh2, w3 = ffn_weights(w_rnd if exact else w_raw)

                def act(ap):
                    return ap if exact else ap.bitcast(F32)

                def gate(i):
                    dve_x2.wait(pe, i)
                    if exact:
                        pe.wait_ge(rounded, 2)
                    for m in range(HC):
                        if m == 1:
                            dve_fin.wait(pe, i - 1)
                        if m >= 4:
                            dve_lo.wait(pe, i, m - 3)
                        for w, bank in zip((w1, w2), PAIRS[m % 4]):
                            for c in range(DC):
                                pe.matmul(bank[:], w[:, c, m * P:(m + 1) * P], act(x2_hi[:, c, :]), start=(c == 0), stop=False)
                                mm = pe.matmul(bank[:], w[:, c, m * P:(m + 1) * P], act(x2_lo[:, c, :]), start=False, stop=(c == DC - 1))
                            pe_ab.add(mm)

                def hidden(i, w, hi, lo, ready, before_, evacuated, done, chunks):
                    for m in chunks:
                        if m < 4:
                            tally_, k = before_(m)
                            tally_.wait(pe, i, k)
                        else:
                            evacuated.wait(pe, i, m - 3)
                        for c in range(HC):
                            if m == 0 and c + 1 > before_(0)[1]:
                                ready.wait(pe, i, c + 1)
                            pe.matmul(F[m % 4][:], w[:, c, m * P:(m + 1) * P], act(hi[:, c, :]), start=(c == 0), stop=False)
                            mm = pe.matmul(F[m % 4][:], w[:, c, m * P:(m + 1) * P], act(lo[:, c, :]), start=False, stop=(c == HC - 1))
                        done.add(mm)

                def hidden1(i, chunks):
                    if exact and 0 in chunks:
                        pe.wait_ge(rounded_dve, 1)
                    hidden(i, wh1, ha_hi, ha_lo, dve_lo, lambda m: (dve_lo, 6), dve_lo1, pe_h1, chunks)

                def hidden2(i, chunks):
                    if exact and 0 in chunks:
                        pe.wait_ge(rounded_dve, 2)
                    hidden(i, wh2, hb_hi, hb_lo, dve_lo1, lambda m: (dve_lo1, m + 5), dve_lo2, pe_h2, chunks)

                def last(i):
                    if exact:
                        pe.wait_ge(rounded_dve, 3)
                    dve_lo2.wait(pe, i, 6)
                    for b in range(NB):
                        bank = F[b // 2][:, (b % 2) * D:(b % 2 + 1) * D]
                        for c in range(HC):
                            if b == 0 and c >= 6:
                                dve_lo2.wait(pe, i, c + 1)
                            pe.matmul(bank, act(ha_hi[:, c, b * P:(b + 1) * P]), w3[:, c, :], start=(c == 0), stop=False)
                            mm = pe.matmul(bank, act(ha_lo[:, c, b * P:(b + 1) * P]), w3[:, c, :], start=False, stop=(c == HC - 1))
                        if b % 2:
                            pe_w3.add(mm)

                with pe.Fori(0, NT - 1) as i:
                    gate(i)
                    hidden1(i, [0])
                    transpose_x(i + 1)
                    hidden1(i, [1, 2])
                    project(i + 1)
                    hidden1(i, range(3, HC))
                    hidden2(i, range(4))
                    project_out(i + 1)
                    hidden2(i, range(4, HC))
                    transpose_x2(i + 1)
                    last(i)
                i = NT - 1
                gate(i)
                hidden1(i, range(HC))
                hidden2(i, range(HC))
                last(i)

            pe.wait_ge(setup_pool, 1)
            transpose_x(0)
            pe.wait_ge(ld_const, 16 * 3)
            project(0)
            project_out(0)
            transpose_x2(0)
            pe.wait_ge(setup_dve, 3)
            pe.matmul(F[0][0:1, 0:1], inexact[:], ones[:], start=True, stop=True).then_inc(flag_sum, 1)
            pe.wait_ge(flag_set, 1)
            flag = pe.value_load(general[0:1, 0:1], min_val=0, max_val=LOW_BITS * P)
            with pe.If(flag > 0):
                mlp(exact=False)
            with pe.Else():
                mlp(exact=True)

        @block.scalar
        def _(act):
            for t in (act_x, act_kvr, act_exp, act_x2, act_silu, act_hi, act_hi1, act_h1, act_hi2, act_h2):
                t.start(act)

            def copy_x(t):
                pool_num.wait(act, t - 1)
                act_x.wait(act, t - 1)
                act_x.add(act.activation(seq[:, :, :, 0:1], carry_x[:], ACT.Copy))
                for c in range(DC):
                    pe_xT.wait(act, t, c + 1)
                    act_x.add(act.activation(now[:, c], A[c][:].rearrange("p (n t) -> p n t", n=n_seq), ACT.Copy))
                act_x.wait(act, t, 3)
                act_x.add(act.activation(carry_x[:], seq[:, :, :, SEG:SEG + 1], ACT.Copy))

            def copy_kvr(t):
                for j in range(3 * DC):
                    which, e = divmod(j, DC)
                    pe_kvr.wait(act, t, j + 1)
                    act_kvr.add(act.activation((k_sb, v_sb, r_sb)[which][:, e, :], KVR_BANK[j][:], ACT.Copy))

            def exps(t):
                for k, (ap, sign) in enumerate(((mix_r, -1.0), (norm_ch, 1.0), (mix_v, 1.0), (mix_k, -1.0))):
                    if k == 0:
                        dve_pre.wait(act, t)
                    act_exp.add(act.activation(ap[:], ap[:], ACT.Exp, scale=sign))
                act_kvr.wait(act, t)
                act_exp.add(act.activation(r_sb[:], r_sb[:], ACT.Exp, scale=-1.0))

            def round_x2(t):
                for c in range(DC):
                    pe_x2T.wait(act, t, c + 1)
                    act_x2.add(act.activation(x2_hi[:, c, :], A[2 + c][:], ACT.Copy))

            def gate(i):
                def silu(m):
                    pe_ab.wait(act, i, 2 * m + 1)
                    if m >= 2:
                        dve_prod.wait(act, i, m - 1)
                    act_silu.add(act.activation(mix_k[:, m % 2, :], PAIRS[m % 4][0][:], ACT.Silu, scale=s1[:, m:m + 1]))

                def hi(m):
                    dve_prod.wait(act, i, m + 1)
                    act_hi.add(act.activation(ha_hi[:, m, :], PAIRS[m % 4][1][:], ACT.Copy))

                for m in range(HC):
                    silu(m)
                    if m:
                        hi(m - 1)
                hi(HC - 1)

            def gelu(i, m, scale, ready, hi, hi_done, done):
                ready.wait(act, i, m + 1)
                hi_done.add(act.activation(hi[:, m, :], F[m % 4][:], ACT.Gelu, scale=scale[:, m:m + 1]))
                hi_done.wait(act, i, m + 1)
                done.add(act.activation(F[m % 4][:], F[m % 4][:], ACT.Gelu, scale=scale[:, m:m + 1]))

            def gelu1(i, m):
                gelu(i, m, sh1, pe_h1, hb_hi, act_hi1, act_h1)

            def gelu2(i, m):
                gelu(i, m, sh2, pe_h2, ha_hi, act_hi2, act_h2)

            act.wait_ge(setup_pool, 2)
            copy_x(0)
            copy_kvr(0)
            exps(0)
            round_x2(0)
            act.wait_ge(flag_set, 1)
            flag = act.value_load(general[0:1, 0:1], min_val=0, max_val=LOW_BITS * P)
            with act.If(flag == 0):
                for j in range(2):
                    act.activation(w_rnd[:, j * W12:(j + 1) * W12], w_raw[:, j * W12:(j + 1) * W12], ACT.Copy).then_inc(rounded, 1)

            with act.Fori(0, NT - 1) as i:
                gate(i)
                gelu1(i, 0)
                copy_x(i + 1)
                gelu1(i, 1)
                gelu1(i, 2)
                copy_kvr(i + 1)
                gelu1(i, 3)
                exps(i + 1)
                for m in range(4, HC):
                    gelu1(i, m)
                for m in range(HC):
                    gelu2(i, m)
                round_x2(i + 1)
            i = NT - 1
            gate(i)
            for m in range(HC):
                gelu1(i, m)
            for m in range(HC):
                gelu2(i, m)

        @block.vector
        def _(dve):
            chain = Chain(ctx, nc, "dve_chain", dve, 41)
            for t in (dve_seed1, dve_seed2, dve_norm1, dve_norm2, dve_mix, dve_pre, dve_q, dve_y, dve_x1, dve_x2,
                      dve_prod, dve_lo, dve_lo1, dve_lo2, dve_fin):
                t.start(dve)

            def statistics(t, src, seed):
                chain.wait(t)
                for b in range(NB):
                    chain.link(dve.bn_stats(stats[:, b, :], src[:, b, :]))
                chain.wait(t)
                stand_alone(dve, spare)
                for b in range(NB):
                    chain.link(dve.bn_aggr(moments[:, b, :], stats[:, b, :]))
                chain.wait(t)
                chain.done(dve.tensor_scalar(var[:], moments[:, :, 1], LN_EPS, None, ALU.add), t)
                chain.done(dve.tensor_scalar(shifted[:], var[:].bitcast(I32), 1, None, ALU.arith_shift_right), t)
                seed.add(dve.tensor_scalar(rstd[:].bitcast(I32), shifted[:], -1.0, float(RSQRT_SEED), ALU.mult, ALU.add))

            def normalise(t, src, refined, done):
                refined.wait(dve, t)
                for b in range(NB):
                    done.add(dve.tensor_scalar(norm_tok[:, b, :], src[:, b, :], moments[:, b, 0:1], rstd[:, b:b + 1],
                                               ALU.subtract, ALU.mult))

            def ln1_statistics(t):
                ld_x.wait(dve, t)
                statistics(t, x_in, dve_seed1)

            def ln1(t):
                normalise(t, x_in, pool_rs1, dve_norm1)

            def mix(t):
                act_x.wait(dve, t)
                st_out.wait(dve, t - 2)
                dve_prod.wait(dve, t - 1)
                chain.done(dve.tensor_tensor(by_seq(norm_ch), now, before, ALU.subtract), t)
                for dst, tm in ((mix_k, tmk), (mix_v, tmv), (mix_r, tmr)):
                    for c in range(DC):
                        dve_mix.add(dve.scalar_tensor_tensor(
                            by_seq(dst[:])[:, c], by_seq(norm_ch)[:, c], tm[:, c:c + 1], before[:, c], ALU.mult, ALU.add))

            def running_max(t):
                act_kvr.wait(dve, t, DC)
                dve_mix.wait(dve, t)
                chain.done(dve.tensor_copy(seq[:, :, :, 0:1], carry_p[:]), t)
                for c in range(DC):
                    for n in range(n_seq):
                        chain.link(dve.tensor_tensor_scan(
                            now[:, c, n, :], decay[:, c:c + 1].broadcast_to([P, SEG]), by_seq(k_sb[:])[:, c, n, :],
                            carry_p[:, c, n, :], ALU.add, ALU.max))
                chain.wait(t)
                chain.link(dve.tensor_copy(carry_p[:], seq[:, :, :, SEG:SEG + 1]))

            def exponents(t):
                k4 = by_seq(k_sb[:])
                pe_kvr.wait(dve, t, DC)
                for c in range(DC):
                    chain.link(dve.scalar_tensor_tensor(by_seq(mix_k[:])[:, c], k4[:, c], first[:, c:c + 1], before[:, c], ALU.add, ALU.subtract))
                for c in range(DC):
                    chain.link(dve.scalar_tensor_tensor(by_seq(norm_ch)[:, c], before[:, c], decay[:, c:c + 1], k4[:, c], ALU.add, ALU.subtract))
                chain.wait(t)
                pe_kvr.wait(dve, t, 2 * DC)
                dve_pre.add(dve.tensor_scalar(mix_v[:], mix_k[:], 0.0, -CLAMP, ALU.min, ALU.max))
                dve_pre.wait(dve, t, 1)
                dve_pre.add(dve.tensor_scalar(mix_k[:], mix_k[:], 0.0, CLAMP, ALU.max, ALU.min))
                pe_kvr.wait(dve, t, 3 * DC)
                dve_pre.add(dve.tensor_scalar(mix_r[:], norm_ch, 0.0, CLAMP, ALU.max, ALU.min))
                dve_pre.wait(dve, t, 3)
                dve_pre.add(dve.tensor_scalar(norm_ch, norm_ch, 0.0, -CLAMP, ALU.min, ALU.max))

            def recurrence(t):
                act_exp.wait(dve, t, 2)
                chain.done(dve.tensor_tensor(mix_r[:], mix_r[:], v_sb[:], ALU.mult), t)
                chain.link(dve.tensor_copy(seq[:, :, :, 0:1], carry_q[:]))
                for c in range(DC):
                    for n in range(n_seq):
                        chain.link(dve.tensor_tensor_scan(
                            now[:, c, n, :], by_seq(norm_ch)[:, c, n, :], by_seq(mix_r[:])[:, c, n, :],
                            carry_q[:, c, n, :], ALU.mult, ALU.add))
                chain.wait(t)
                dve_q.add(dve.tensor_copy(carry_q[:], seq[:, :, :, SEG:SEG + 1]))

            def denominator(t):
                act_exp.wait(dve, t)
                chain.done(dve.scalar_tensor_tensor(k_sb[:], mix_k[:], WKV_EPS, mix_v[:], ALU.add, ALU.add), t)
                chain.done(dve.scalar_tensor_tensor(r_sb[:], r_sb[:], 1.0, k_sb[:], ALU.add, ALU.mult), t)

            def invert(t, c):
                chain.link(dve.reciprocal(k_sb[:, c, :], r_sb[:, c, :]))

            def weigh(t):
                pool_num.wait(dve, t)
                chain.wait(t)
                dve_y.add(dve.tensor_tensor(v_sb[:], mix_r[:], k_sb[:], ALU.mult))

            def residual(t):
                pool_x1.wait(dve, t - 1)
                for j in range(2):
                    pe_wo.wait(dve, t, j + 1)
                    dve_x1.add(dve.tensor_tensor(x1_next[:, 2 * j:2 * j + 2, :], A[j][:].rearrange("p (b d) -> p b d", b=2),
                                                 x_in[:, 2 * j:2 * j + 2, :], ALU.add))

            def ln2_statistics(t):
                dve_x1.wait(dve, t)
                statistics(t, x1_next, dve_seed2)

            def ln2(t):
                normalise(t, x1_next, pool_rs2, dve_norm2)

            def rest_x2(t):
                for c in range(DC):
                    act_x2.wait(dve, t, c + 1)
                    dve_x2.add(dve.tensor_tensor(x2_lo[:, c, :], A[2 + c][:], x2_hi[:, c, :].bitcast(F32), ALU.subtract))

            def prod(i, m):
                act_silu.wait(dve, i, m + 1)
                pe_ab.wait(dve, i, 2 * m + 2)
                b = PAIRS[m % 4][1]
                dve_prod.add(dve.scalar_tensor_tensor(b[:], b[:], s2[:, m:m + 1], mix_k[:, m % 2, :], ALU.mult, ALU.mult))

            def lo(i, m):
                act_hi.wait(dve, i, m + 1)
                dve_lo.add(dve.tensor_tensor(ha_lo[:, m, :], PAIRS[m % 4][1][:], ha_hi[:, m, :].bitcast(F32), ALU.subtract))

            def lo1(i, m):
                act_h1.wait(dve, i, m + 1)
                dve_lo1.add(dve.tensor_tensor(hb_lo[:, m, :], F[m % 4][:], hb_hi[:, m, :].bitcast(F32), ALU.subtract))

            def lo2(i, m):
                act_h2.wait(dve, i, m + 1)
                dve_lo2.add(dve.tensor_tensor(ha_lo[:, m, :], F[m % 4][:], ha_hi[:, m, :].bitcast(F32), ALU.subtract))

            def finish(i):
                st_out.wait(dve, i - 1)
                for j in range(2):
                    pe_w3.wait(dve, i, j + 1)
                    dve_fin.add(dve.tensor_tensor(out_tok[:, 2 * j:2 * j + 2, :], F[j][:].rearrange("p (b d) -> p b d", b=2),
                                                  s3_row[:].rearrange("p (a d) -> p a d", a=1).broadcast_to([P, 2, D]), ALU.mult))

            dve.memset(ones[:], 1.0).then_inc(setup_dve, 1)
            ln1_statistics(0)
            ln1(0)
            dve.wait_ge(ld_const, 16 * 3)
            dve.wait_ge(setup_pool, 2)
            mix(0)
            running_max(0)
            exponents(0)
            recurrence(0)
            denominator(0)
            for c in range(DC):
                invert(0, c)
            weigh(0)
            residual(0)
            ln2_statistics(0)
            ln2(0)
            rest_x2(0)
            chain.end_tile()
            w_bits = w_raw[:].bitcast(I32)
            CHUNK = W12
            n_chunks = NW // CHUNK
            seen = ctx.enter_context(nc.semaphore("seen"))
            dve.wait_ge(ld_w, 16 * 5)
            dve.tensor_tensor(check[:], w_bits[:, 0:CHUNK], w_bits[:, CHUNK:2 * CHUNK], ALU.bitwise_or).then_inc(seen, 1)
            for j in range(2, n_chunks):
                dve.wait_ge(seen, j - 1)
                dve.tensor_tensor(check[:], check[:], w_bits[:, j * CHUNK:(j + 1) * CHUNK], ALU.bitwise_or).then_inc(seen, 1)
            dve.wait_ge(seen, n_chunks - 1)
            dve.tensor_scalar(check[:], check[:], LOW_BITS, None, ALU.bitwise_and).then_inc(seen, 1)
            dve.wait_ge(seen, n_chunks)
            dve.tensor_reduce(inexact[:], check[:], AX_X, ALU.max).then_inc(setup_dve, 2)
            dve.wait_ge(flag_sum, 1)
            dve.tensor_copy(general[:], F[0][0:1, 0:1]).then_inc(flag_set, 1)
            dve.wait_ge(flag_set, 1)
            flag = dve.value_load(general[0:1, 0:1], min_val=0, max_val=LOW_BITS * P)
            with dve.If(flag == 0):
                a = 2 * W12
                for n in (HH, HH, W3):
                    dve.tensor_copy(w_rnd[:, a:a + n], w_raw[:, a:a + n]).then_inc(rounded_dve, 1)
                    a += n

            def gate(i, t):
                prod(i, 0)
                for m in range(1, HC):
                    prod(i, m)
                    lo(i, m - 1)
                    if m == 2 and t is not None:
                        ln1_statistics(t)
                    if m == 5 and t is not None:
                        ln1(t)
                lo(i, HC - 1)

            with dve.Fori(0, NT - 1) as i:
                t = i + 1
                gate(i, t)
                lo1(i, 0)
                mix(t)
                lo1(i, 1)
                lo1(i, 2)
                running_max(t)
                exponents(t)
                lo1(i, 3)
                recurrence(t)
                denominator(t)
                invert(t, 0)
                for m in range(4, HC):
                    lo1(i, m)
                invert(t, 1)
                weigh(t)
                for m in range(4):
                    lo2(i, m)
                residual(t)
                ln2_statistics(t)
                lo2(i, 4)
                ln2(t)
                for m in range(5, HC):
                    lo2(i, m)
                rest_x2(t)
                finish(i)
                chain.end_tile()
            i = NT - 1
            gate(i, None)
            for m in range(HC):
                lo1(i, m)
            for m in range(HC):
                lo2(i, m)
            finish(i)

        @block.gpsimd
        def _(pool):
            for t in (pool_rs1, pool_rs2, pool_num, pool_out, pool_x1):
                t.start(pool)
            chain = Chain(ctx, nc, "pool_chain", pool, 2 * (4 * NEWTON_STEPS - 1) + 2)

            def refine(t, seed, done):
                seed.wait(pool, t)
                for step in range(NEWTON_STEPS):
                    chain.done(pool.tensor_tensor(newton[:, 0, :], rstd[:], rstd[:], ALU.mult), t)
                    chain.link(pool.tensor_tensor(newton[:, 1, :], newton[:, 0, :], var[:], ALU.mult))
                    chain.wait(t)
                    stand_alone(pool, spare)
                    chain.done(pool.tensor_scalar(newton[:, 0, :], newton[:, 1, :], -0.5, 1.5, ALU.mult, ALU.add), t)
                    y = pool.tensor_tensor(rstd[:], rstd[:], newton[:, 0, :], ALU.mult)
                    if step < NEWTON_STEPS - 1:
                        chain.done(y, t)
                    else:
                        done.add(y)

            def numerator(t):
                act_exp.wait(pool, t, 4)
                dve_q.wait(pool, t)
                chain.link(pool.tensor_tensor(v_sb[:], mix_v[:], v_sb[:], ALU.mult))
                chain.done(pool.tensor_tensor(by_seq(norm_ch), by_seq(mix_k[:]), before, ALU.mult), t)
                pool_num.add(pool.tensor_tensor(mix_r[:], v_sb[:], norm_ch, ALU.add))

            def add_x1(i):
                pool_x1.wait(pool, i)
                for j in range(2):
                    dve_fin.wait(pool, i, j + 1)
                    o = out_tok[:, 2 * j:2 * j + 2, :]
                    pool_out.add(pool.tensor_tensor(o, o, x1[:, 2 * j:2 * j + 2, :], ALU.add))

            def keep_x1(t):
                dve_x1.wait(pool, t)
                pool_out.wait(pool, t - 1)
                stand_alone(pool, spare)
                pool_x1.add(pool.tensor_copy(x1[:], x1_next[:]))

            pool.memset(ident[:], 0.0).then_inc(setup_ident, 1)
            pool.wait_ge(setup_ident, 1)
            pool.affine_select(out=ident[:], in_=ident[:], compare_op=ALU.not_equal, fill=1.0, base=0,
                               pattern=[[-1, P]], channel_multiplier=1).then_inc(setup_pool, 1)
            pool.memset(carry_x[:], 0.0)
            pool.memset(carry_q[:], 0.0)
            pool.memset(carry_p[:], LOWEST).then_inc(setup_pool, 1)
            refine(0, dve_seed1, pool_rs1)
            numerator(0)
            refine(0, dve_seed2, pool_rs2)
            keep_x1(0)
            chain.end_tile()
            with pool.Fori(0, NT - 1) as i:
                refine(i + 1, dve_seed1, pool_rs1)
                numerator(i + 1)
                refine(i + 1, dve_seed2, pool_rs2)
                add_x1(i)
                keep_x1(i + 1)
                chain.end_tile()
            add_x1(NT - 1)


_ORDER = ("x", "vectors", "w_mix", "w_ffn", "s3")


def kernel(**inputs):
    import concourse.bacc as bacc
    from concourse.bass_utils import run_bass_kernel_spmd

    a = {k.removeprefix("L0_"): np.asarray(v) for k, v in inputs.items()}

    def columns(v):
        return v.reshape(-1, P).T

    def by_input(w):
        return w.T.reshape(-1, P, w.shape[0]).transpose(1, 0, 2)

    arrays = {
        "x": a["attn_x"],
        "vectors": np.concatenate([columns(a[k]) for k in (
            "attn_time_mix_k", "attn_time_mix_v", "attn_time_mix_r", "attn_time_decay", "attn_time_first",
            "ffn_w1_s", "ffn_w2_s", "ffn_h1_s", "ffn_h2_s")], axis=1),
        "w_mix": np.stack([by_input(a[f"attn_W_{k}"]) for k in "kvro"], axis=1),
        "w_ffn": np.concatenate([by_input(a[f"ffn_{k}_w"]).reshape(P, -1) for k in ("w1", "w2", "h1", "h2", "w3")], axis=1),
        "s3": a["ffn_w3_s"].reshape(1, -1),
    }
    arrays = {f"in_{k}": np.ascontiguousarray(v) for k, v in arrays.items()}
    nc = bacc.Bacc("TRN2", target_bir_lowering=False, num_devices=1)
    args = [nc.dram_tensor(f"in_{k}", arrays[f"in_{k}"].shape, F32, kind="ExternalInput").ap() for k in _ORDER]
    args.append(nc.dram_tensor("out", a["attn_x"].shape, F32, kind="ExternalOutput").ap())
    build(nc, *args)
    r = run_bass_kernel_spmd(nc, [arrays], core_ids=[0])
    return r.results[0]["out"]
```

```python
from contextlib import ExitStack

import numpy as np

import concourse.bass as bass
from concourse import mybir

F32 = mybir.dt.float32
F32R = mybir.dt.float32r
BF16 = mybir.dt.bfloat16
U16 = mybir.dt.uint16
I32 = mybir.dt.int32
ALU = mybir.AluOpType
ACT = mybir.ActivationFunctionType
AX_X = mybir.AxisListType.X

P = 128
LN_EPS = 1e-5
WKV_EPS = 1e-9
CLAMP = 30.0
LOWEST = float(np.finfo(np.float32).min)
RSQRT_SEED = 0x5F3759DF
NEWTON_STEPS = 3


def stand_alone(eng, spare):
    eng.sem_inc(spare, 1)


class Tally:

    def __init__(self, ctx, nc, name, per, unit=1):
        self.sem = ctx.enter_context(nc.semaphore(name))
        self.per, self.unit = per, unit

    def start(self, eng):
        eng.sem_inc(self.sem, self.per * self.unit)

    def wait(self, eng, tile, k=None):
        k = self.per if k is None else k
        eng.wait_ge(self.sem, tile * (self.per * self.unit) + (self.per + k) * self.unit)

    def add(self, instruction):
        instruction.then_inc(self.sem, self.unit)
        return instruction


class Chain:

    def __init__(self, ctx, nc, name, eng, per):
        self.sem = ctx.enter_context(nc.semaphore(name))
        self.eng, self.per, self.n = eng, per, 0

    def link(self, instruction):
        instruction.then_inc(self.sem, 1)
        self.n += 1

    def wait(self, tile):
        self.eng.wait_ge(self.sem, tile * self.per + self.n)

    def done(self, instruction, tile):
        self.link(instruction)
        self.wait(tile)

    def end_tile(self):
        assert self.n == self.per, (self.n, self.per)
        self.n = 0


def build(nc, x, vectors, w_mix, w_ffn, s3, out):
    n_seq, T, D = x.shape
    DC = D // P
    H = 1024
    HC = H // P
    TILE = 512
    SEG = TILE // n_seq
    HALVES = SEG // P
    NB = TILE // P
    NT = T // SEG
    SW = DC * TILE
    W12, HH, W3 = DC * H, HC * H, HC * D
    assert vectors.shape[1] == 5 * DC + 4 * HC and w_ffn.shape[1] == 2 * W12 + 2 * HH + W3

    x_tiles = x.rearrange("n (i h p) d -> n i p h d", h=HALVES, p=P)
    out_tiles = out.rearrange("n (i h p) d -> n i p h d", h=HALVES, p=P)

    with ExitStack() as ctx:
        def sb(name, shape, dt=F32):
            return ctx.enter_context(nc.sbuf_tensor(name, shape, dt))

        def overlay(name, shape, dt):
            with nc.sbuf_tensor(name, shape, dt) as t:
                return t

        def tally(name, per, unit=1):
            return Tally(ctx, nc, name, per, unit)

        NW = 2 * W12 + 2 * HH + W3
        w_raw = overlay("w_raw", [P, NW], F32)
        w_rnd = sb("w_rnd", [P, NW], F32R)
        wm = sb("wm", [P, 4, DC, D])
        x_in = sb("x_in", [P, NB, D])
        norm = sb("norm", [P, NB * D])
        seq = sb("seq", [P, DC, n_seq, SEG + 1])
        mix_k = sb("mix_k", [P, DC, TILE])
        mix_v = sb("mix_v", [P, DC, TILE])
        mix_r = sb("mix_r", [P, DC, TILE])
        x2_hi = overlay("x2_hi", [P, DC, TILE], F32R)
        k_sb = sb("k_sb", [P, DC, TILE])
        x2_lo = overlay("x2_lo", [P, DC, TILE], F32R)
        r_sb = sb("r_sb", [P, DC, TILE])
        v_sb = sb("v_sb", [P, DC, TILE])
        x1_next = sb("x1_next", [P, NB, D])
        x1 = sb("x1", [P, NB, D])
        unused = overlay("unused", [P, NW], BF16)
        ha_hi = sb("ha_hi", [P, HC, TILE], F32R)
        ha_lo = sb("ha_lo", [P, HC, TILE], F32R)
        hb_hi = sb("hb_hi", [P, HC, TILE], F32R)
        hb_lo = sb("hb_lo", [P, HC, TILE], F32R)
        vec = sb("vec", [P, vectors.shape[1]])
        s3_row = sb("s3_row", [P, D])
        ident = sb("ident", [P, P])
        carry_x = sb("carry_x", [P, DC, n_seq, 1])
        carry_p = sb("carry_p", [P, DC, n_seq, 1])
        carry_q = sb("carry_q", [P, DC, n_seq, 1])
        stats = sb("stats", [P, NB, 6])
        moments = sb("moments", [P, NB, 2])
        var = sb("var", [P, NB])
        shifted = sb("shifted", [P, NB], I32)
        rstd = sb("rstd", [P, NB])
        newton = sb("newton", [P, 2, NB])
        low_sums = sb("low_sums", [P, 5])
        low_max = sb("low_max", [1, 1])
        ones = sb("ones", [P, 1])
        general = sb("general", [1, 1], I32)

        F = [ctx.enter_context(nc.psum_tensor(f"ffn{i}", [P, 512], F32)) for i in range(4)]
        A = [ctx.enter_context(nc.psum_tensor(f"att{i}", [P, 512], F32)) for i in range(4)]
        PAIRS = [(F[2], F[3]), (F[0], F[1]), (A[0], A[1]), (A[2], A[3])]
        KVR_BANK = [A[2], A[3], A[0], A[1], A[2], A[3]]

        tmk, tmv, tmr, decay, first = (vec[:, DC * j:DC * (j + 1)] for j in range(5))
        s1, s2, sh1, sh2 = (vec[:, 5 * DC + HC * j:5 * DC + HC * (j + 1)] for j in range(4))
        norm_tok = norm[:].rearrange("p (b d) -> p b d", b=NB)
        norm_ch = norm[:].rearrange("p (c t) -> p c t", c=DC)
        out_tok = mix_v[:].rearrange("p c t -> p (c t)").rearrange("p (b d) -> p b d", b=NB)

        def by_seq(ap):
            return ap.rearrange("p c (n t) -> p c n t", n=n_seq)

        now, before = seq[:, :, :, 1:], seq[:, :, :, 0:SEG]

        def ffn_weights(w):
            a = 0
            parts = []
            for n, c in ((W12, DC), (W12, DC), (HH, HC), (HH, HC), (W3, HC)):
                parts.append(w[:, a:a + n].rearrange("p (c o) -> p c o", c=c))
                a += n
            return parts

        ld_const = ctx.enter_context(nc.semaphore("ld_const"))
        ld_w = [ctx.enter_context(nc.semaphore(f"ld_{k}")) for k in ("w1", "w2", "h1", "h2", "w3")]
        setup_pool = ctx.enter_context(nc.semaphore("setup_pool"))
        setup_dve = ctx.enter_context(nc.semaphore("setup_dve"))
        setup_ident = ctx.enter_context(nc.semaphore("setup_ident"))
        spare = ctx.enter_context(nc.semaphore("spare"))
        flag_sum = ctx.enter_context(nc.semaphore("flag_sum"))
        flag_set = ctx.enter_context(nc.semaphore("flag_set"))
        low_done = ctx.enter_context(nc.semaphore("low_done"))
        flag_max = ctx.enter_context(nc.semaphore("flag_max"))
        rounded_12, rounded_h1, rounded_h2_3 = (ctx.enter_context(nc.semaphore(n)) for n in (
            "rounded_12", "rounded_h1", "rounded_h2_3"))
        ld_x = tally("ld_x", n_seq, 16)
        st_out = tally("st_out", n_seq, 16)
        pe_xT, pe_kvr, pe_wo, pe_x2T = (tally(n, k) for n, k in (("pe_xT", DC), ("pe_kvr", 3 * DC), ("pe_wo", 2), ("pe_x2T", DC)))
        pe_a, pe_b, pe_h1, pe_h2, pe_w3 = (tally(n, k) for n, k in (("pe_a", HC), ("pe_b", HC), ("pe_h1", HC), ("pe_h2", HC), ("pe_w3", 2)))
        act_x, act_kvr, act_exp, act_x2 = (tally(n, k) for n, k in (("act_x", 4), ("act_kvr", 3 * DC), ("act_exp", 5), ("act_x2", DC)))
        act_silu, act_hi, act_hi1, act_h1, act_hi2, act_h2 = (tally(n, HC) for n in ("act_silu", "act_hi", "act_hi1", "act_h1", "act_hi2", "act_h2"))
        dve_seed1, dve_seed2, dve_norm1, dve_norm2 = (tally(n, k) for n, k in (("dve_seed1", 1), ("dve_seed2", 1), ("dve_norm1", NB), ("dve_norm2", NB)))
        dve_mix, dve_pre, dve_q, dve_y, dve_x1, dve_x2 = (tally(n, k) for n, k in (
            ("dve_mix", 3 * DC), ("dve_pre", 4), ("dve_q", 1), ("dve_y", 1), ("dve_x1", 2), ("dve_x2", DC)))
        dve_prod, dve_lo, dve_lo1, dve_lo2, dve_fin = (tally(n, k) for n, k in (
            ("dve_prod", HC), ("dve_lo", HC), ("dve_lo1", HC), ("dve_lo2", HC), ("dve_fin", 2)))
        pool_rs1, pool_rs2, pool_num, pool_out, pool_x1 = (tally(n, k) for n, k in (
            ("pool_rs1", 1), ("pool_rs2", 1), ("pool_num", 1), ("pool_out", 2), ("pool_x1", 1)))

        block = ctx.enter_context(nc.Block())

        @block.sync
        def _(sp):
            for t in (ld_x, st_out):
                t.start(sp)

            def load_x(t):
                dve_x1.wait(sp, t - 1)
                for n in range(n_seq):
                    ld_x.add(sp.dma_start(x_in[:, HALVES * n:HALVES * (n + 1), :], x_tiles[n, t]))

            def store(i):
                for j in range(2):
                    pool_out.wait(sp, i, j + 1)
                    st_out.add(sp.dma_start(out_tiles[j, i], out_tok[:, HALVES * j:HALVES * (j + 1), :]))

            load_x(0)
            sp.dma_start(vec[:], vectors).then_inc(ld_const, 16)
            sp.dma_start(wm[:], w_mix).then_inc(ld_const, 16)
            sp.dma_start(s3_row[:], s3.broadcast_to([P, D])).then_inc(ld_const, 16)
            a = 0
            for n, loaded in zip((W12, W12, HH, HH, W3), ld_w):
                sp.dma_start(w_raw[:, a:a + n], w_ffn[:, a:a + n]).then_inc(loaded, 16)
                a += n
            with sp.Fori(0, NT - 1) as i:
                load_x(i + 1)
                store(i)
            store(NT - 1)
            st_out.wait(sp, NT - 1)

        @block.tensor
        def _(pe):
            for t in (pe_xT, pe_kvr, pe_wo, pe_x2T, pe_a, pe_b, pe_h1, pe_h2, pe_w3):
                t.start(pe)

            def transpose_x(t):
                dve_norm1.wait(pe, t)
                for c in range(DC):
                    for b in range(NB):
                        mm = pe.transpose(A[c][:, b * P:(b + 1) * P], norm_tok[:, b, c * P:(c + 1) * P], ident[:])
                    pe_xT.add(mm)

            def project(t):
                for j in range(3 * DC):
                    which, e = divmod(j, DC)
                    src = (mix_k, mix_v, mix_r)[which]
                    dve_mix.wait(pe, t, j // DC * DC + DC)
                    if j >= 4:
                        act_kvr.wait(pe, t, j - 3)
                    for c in range(DC):
                        mm = pe.matmul(KVR_BANK[j][:], wm[:, which, c, e * P:(e + 1) * P], src[:, c, :],
                                       start=(c == 0), stop=(c == DC - 1))
                    pe_kvr.add(mm)

            def project_out(t):
                dve_y.wait(pe, t)
                for b in range(NB):
                    for c in range(DC):
                        mm = pe.matmul(A[b // 2][:, (b % 2) * D:(b % 2 + 1) * D], v_sb[:, c, b * P:(b + 1) * P],
                                       wm[:, 3, c, :], start=(c == 0), stop=(c == DC - 1))
                    if b % 2:
                        pe_wo.add(mm)

            def transpose_x2(t):
                dve_norm2.wait(pe, t)
                for c in range(DC):
                    for b in range(NB):
                        mm = pe.transpose(A[2 + c][:, b * P:(b + 1) * P], norm_tok[:, b, c * P:(c + 1) * P], ident[:])
                    pe_x2T.add(mm)

            def mlp(exact):
                w1, w2, wh1, wh2, w3 = ffn_weights(w_rnd if exact else w_raw)

                def act(ap):
                    return ap if exact else ap.bitcast(F32)

                def gate(i):
                    dve_x2.wait(pe, i)
                    if exact:
                        pe.wait_ge(rounded_12, 1)
                    order = [(m, j) for m in range(HC - 2) for j in range(2)] + [(m, j) for j in range(2) for m in (HC - 2, HC - 1)]
                    for m, j in order:
                        if m == 1 and j == 0:
                            dve_fin.wait(pe, i - 1)
                        if m >= 4 and j == 0:
                            dve_lo.wait(pe, i, m - 3)
                        for w, bank in (((w1, w2)[j], PAIRS[m % 4][j]),):
                            for c in range(DC):
                                pe.matmul(bank[:], w[:, c, m * P:(m + 1) * P], act(x2_hi[:, c, :]), start=(c == 0), stop=False)
                                mm = pe.matmul(bank[:], w[:, c, m * P:(m + 1) * P], act(x2_lo[:, c, :]), start=False, stop=(c == DC - 1))
                            (pe_a if w is w1 else pe_b).add(mm)

                def hidden(i, w, hi, lo, hi_ready, ready, before_, evacuated, done, chunks):
                    for m in chunks:
                        if m < 4:
                            tally_, k = before_(m)
                            tally_.wait(pe, i, k)
                        else:
                            evacuated.wait(pe, i, m - 3)
                        for c in range(HC):
                            new = m == 0 and c + 1 > before_(0)[1]
                            if new:
                                hi_ready.wait(pe, i, c + 1)
                            pe.matmul(F[m % 4][:], w[:, c, m * P:(m + 1) * P], act(hi[:, c, :]), start=(c == 0), stop=False)
                            if new:
                                ready.wait(pe, i, c + 1)
                            mm = pe.matmul(F[m % 4][:], w[:, c, m * P:(m + 1) * P], act(lo[:, c, :]), start=False, stop=(c == HC - 1))
                        done.add(mm)

                def hidden1(i, chunks):
                    if exact and 0 in chunks:
                        pe.wait_ge(rounded_h1, 1)
                    hidden(i, wh1, ha_hi, ha_lo, act_hi, dve_lo, lambda m: (dve_lo, 6), dve_lo1, pe_h1, chunks)

                def hidden2(i, chunks):
                    if exact and 0 in chunks:
                        pe.wait_ge(rounded_h2_3, 1)
                    hidden(i, wh2, hb_hi, hb_lo, act_hi1, dve_lo1, lambda m: (dve_lo1, m + 5), dve_lo2, pe_h2, chunks)

                def last(i):
                    if exact:
                        pe.wait_ge(rounded_h2_3, 2)
                    dve_lo2.wait(pe, i, 6)
                    for b in range(NB):
                        bank = F[b // 2][:, (b % 2) * D:(b % 2 + 1) * D]
                        for c in range(HC):
                            if b == 0 and c >= 6:
                                dve_lo2.wait(pe, i, c + 1)
                            pe.matmul(bank, act(ha_hi[:, c, b * P:(b + 1) * P]), w3[:, c, :], start=(c == 0), stop=False)
                            mm = pe.matmul(bank, act(ha_lo[:, c, b * P:(b + 1) * P]), w3[:, c, :], start=False, stop=(c == HC - 1))
                        if b % 2:
                            pe_w3.add(mm)

                with pe.Fori(0, NT - 1) as i:
                    gate(i)
                    hidden1(i, [0, 1, 2])
                    transpose_x(i + 1)
                    hidden1(i, [3, 4])
                    project(i + 1)
                    hidden1(i, range(5, HC))
                    hidden2(i, range(5))
                    project_out(i + 1)
                    hidden2(i, range(5, HC))
                    transpose_x2(i + 1)
                    last(i)
                i = NT - 1
                gate(i)
                hidden1(i, range(HC))
                hidden2(i, range(HC))
                last(i)

            pe.wait_ge(setup_pool, 1)
            transpose_x(0)
            pe.wait_ge(ld_const, 16 * 3)
            project(0)
            project_out(0)
            pe.wait_ge(setup_dve, 1)
            pe.wait_ge(low_done, 5)
            pe.matmul(F[0][0:1, 0:5], ones[:], low_sums[:], start=True, stop=True).then_inc(flag_sum, 1)
            transpose_x2(0)
            pe.wait_ge(flag_set, 1)
            flag = pe.value_load(general[0:1, 0:1], min_val=0, max_val=1)
            with pe.If(flag > 0):
                mlp(exact=False)
            with pe.Else():
                mlp(exact=True)

        @block.scalar
        def _(act):
            for t in (act_x, act_kvr, act_exp, act_x2, act_silu, act_hi, act_hi1, act_h1, act_hi2, act_h2):
                t.start(act)

            def copy_x(t):
                pool_num.wait(act, t - 1)
                act_x.wait(act, t - 1)
                act_x.add(act.activation(seq[:, :, :, 0:1], carry_x[:], ACT.Copy))
                for c in range(DC):
                    pe_xT.wait(act, t, c + 1)
                    act_x.add(act.activation(now[:, c], A[c][:].rearrange("p (n t) -> p n t", n=n_seq), ACT.Copy))
                act_x.wait(act, t, 3)
                act_x.add(act.activation(carry_x[:], seq[:, :, :, SEG:SEG + 1], ACT.Copy))

            def copy_kvr(t):
                for j in range(3 * DC):
                    which, e = divmod(j, DC)
                    pe_kvr.wait(act, t, j + 1)
                    act_kvr.add(act.activation((k_sb, v_sb, r_sb)[which][:, e, :], KVR_BANK[j][:], ACT.Copy))

            def exps(t):
                for k, (ap, sign) in enumerate(((mix_r, -1.0), (norm_ch, 1.0), (mix_v, 1.0), (mix_k, -1.0))):
                    if k == 0:
                        dve_pre.wait(act, t)
                    act_exp.add(act.activation(ap[:], ap[:], ACT.Exp, scale=sign))
                act_kvr.wait(act, t)
                act_exp.add(act.activation(r_sb[:], r_sb[:], ACT.Exp, scale=-1.0))

            def round_x2(t):
                for c in range(DC):
                    pe_x2T.wait(act, t, c + 1)
                    act_x2.add(act.activation(x2_hi[:, c, :], A[2 + c][:], ACT.Copy))

            def gate(i):
                def silu(m):
                    pe_a.wait(act, i, m + 1)
                    if m >= 2:
                        dve_prod.wait(act, i, m - 1)
                    act_silu.add(act.activation(mix_k[:, m % 2, :], PAIRS[m % 4][0][:], ACT.Silu, scale=s1[:, m:m + 1]))

                def hi(m):
                    dve_prod.wait(act, i, m + 1)
                    act_hi.add(act.activation(ha_hi[:, m, :], PAIRS[m % 4][1][:], ACT.Copy))

                silu(0)
                for m in range(1, HC):
                    silu(m)
                    hi(m - 1)
                hi(HC - 1)

            def gelu(i, m, scale, ready, hi, hi_done, done):
                ready.wait(act, i, m + 1)
                hi_done.add(act.activation(hi[:, m, :], F[m % 4][:], ACT.Gelu, scale=scale[:, m:m + 1]))
                hi_done.wait(act, i, m + 1)
                done.add(act.activation(F[m % 4][:], F[m % 4][:], ACT.Gelu, scale=scale[:, m:m + 1]))

            def gelu1(i, m):
                gelu(i, m, sh1, pe_h1, hb_hi, act_hi1, act_h1)

            def gelu2(i, m):
                gelu(i, m, sh2, pe_h2, ha_hi, act_hi2, act_h2)

            act.wait_ge(setup_pool, 2)
            copy_x(0)
            copy_kvr(0)
            exps(0)
            halves = w_raw[:].bitcast(U16).rearrange("p (n two) -> p n two", two=2)[:, :, 0]
            a = 0
            for k, n in enumerate((W12, W12, HH, HH, W3)):
                act.wait_ge(ld_w[k], 16)
                act.activation(unused[:, a:a + n], halves[:, a:a + n], ACT.Copy,
                               accum_out=low_sums[:, k:k + 1]).then_inc(low_done, 1)
                a += n
            act.wait_ge(flag_set, 1)
            flag = act.value_load(general[0:1, 0:1], min_val=0, max_val=1)
            round_x2(0)
            with act.If(flag == 0):
                a = 2 * W12
                act.activation(w_rnd[:, a:a + HH], w_raw[:, a:a + HH], ACT.Copy).then_inc(rounded_h1, 1)

            with act.Fori(0, NT - 1) as i:
                gate(i)
                gelu1(i, 0)
                gelu1(i, 1)
                gelu1(i, 2)
                copy_x(i + 1)
                gelu1(i, 3)
                gelu1(i, 4)
                copy_kvr(i + 1)
                exps(i + 1)
                for m in range(5, HC):
                    gelu1(i, m)
                for m in range(HC):
                    gelu2(i, m)
                round_x2(i + 1)
            i = NT - 1
            gate(i)
            for m in range(HC):
                gelu1(i, m)
            for m in range(HC):
                gelu2(i, m)

        @block.vector
        def _(dve):
            chain = Chain(ctx, nc, "dve_chain", dve, 41)
            for t in (dve_seed1, dve_seed2, dve_norm1, dve_norm2, dve_mix, dve_pre, dve_q, dve_y, dve_x1, dve_x2,
                      dve_prod, dve_lo, dve_lo1, dve_lo2, dve_fin):
                t.start(dve)

            def statistics(t, src, seed):
                chain.wait(t)
                for b in range(NB):
                    chain.link(dve.bn_stats(stats[:, b, :], src[:, b, :]))
                chain.wait(t)
                stand_alone(dve, spare)
                for b in range(NB):
                    chain.link(dve.bn_aggr(moments[:, b, :], stats[:, b, :]))
                chain.wait(t)
                chain.done(dve.tensor_scalar(var[:], moments[:, :, 1], LN_EPS, None, ALU.add), t)
                chain.done(dve.tensor_scalar(shifted[:], var[:].bitcast(I32), 1, None, ALU.arith_shift_right), t)
                seed.add(dve.tensor_scalar(rstd[:].bitcast(I32), shifted[:], -1.0, float(RSQRT_SEED), ALU.mult, ALU.add))

            def normalise(t, src, refined, done):
                refined.wait(dve, t)
                for b in range(NB):
                    done.add(dve.tensor_scalar(norm_tok[:, b, :], src[:, b, :], moments[:, b, 0:1], rstd[:, b:b + 1],
                                               ALU.subtract, ALU.mult))

            def ln1_statistics(t):
                ld_x.wait(dve, t)
                statistics(t, x_in, dve_seed1)

            def ln1(t):
                normalise(t, x_in, pool_rs1, dve_norm1)

            def mix(t):
                act_x.wait(dve, t)
                st_out.wait(dve, t - 2)
                dve_prod.wait(dve, t - 1)
                chain.done(dve.tensor_tensor(by_seq(norm_ch), now, before, ALU.subtract), t)
                for dst, tm in ((mix_k, tmk), (mix_v, tmv), (mix_r, tmr)):
                    for c in range(DC):
                        dve_mix.add(dve.scalar_tensor_tensor(
                            by_seq(dst[:])[:, c], by_seq(norm_ch)[:, c], tm[:, c:c + 1], before[:, c], ALU.mult, ALU.add))

            def running_max(t):
                act_kvr.wait(dve, t, DC)
                dve_mix.wait(dve, t)
                chain.done(dve.tensor_copy(seq[:, :, :, 0:1], carry_p[:]), t)
                for c in range(DC):
                    for n in range(n_seq):
                        chain.link(dve.tensor_tensor_scan(
                            now[:, c, n, :], decay[:, c:c + 1].broadcast_to([P, SEG]), by_seq(k_sb[:])[:, c, n, :],
                            carry_p[:, c, n, :], ALU.add, ALU.max))
                chain.wait(t)
                chain.link(dve.tensor_copy(carry_p[:], seq[:, :, :, SEG:SEG + 1]))

            def exponents(t):
                k4 = by_seq(k_sb[:])
                pe_kvr.wait(dve, t, DC)
                for c in range(DC):
                    chain.link(dve.scalar_tensor_tensor(by_seq(mix_k[:])[:, c], k4[:, c], first[:, c:c + 1], before[:, c], ALU.add, ALU.subtract))
                for c in range(DC):
                    chain.link(dve.scalar_tensor_tensor(by_seq(norm_ch)[:, c], before[:, c], decay[:, c:c + 1], k4[:, c], ALU.add, ALU.subtract))
                chain.wait(t)
                pe_kvr.wait(dve, t, 2 * DC)
                dve_pre.add(dve.tensor_scalar(mix_v[:], mix_k[:], 0.0, -CLAMP, ALU.min, ALU.max))
                dve_pre.wait(dve, t, 1)
                dve_pre.add(dve.tensor_scalar(mix_k[:], mix_k[:], 0.0, CLAMP, ALU.max, ALU.min))
                pe_kvr.wait(dve, t, 3 * DC)
                dve_pre.add(dve.tensor_scalar(mix_r[:], norm_ch, 0.0, CLAMP, ALU.max, ALU.min))
                dve_pre.wait(dve, t, 3)
                dve_pre.add(dve.tensor_scalar(norm_ch, norm_ch, 0.0, -CLAMP, ALU.min, ALU.max))

            def recurrence(t):
                act_exp.wait(dve, t, 2)
                chain.done(dve.tensor_tensor(mix_r[:], mix_r[:], v_sb[:], ALU.mult), t)
                chain.link(dve.tensor_copy(seq[:, :, :, 0:1], carry_q[:]))
                for c in range(DC):
                    for n in range(n_seq):
                        chain.link(dve.tensor_tensor_scan(
                            now[:, c, n, :], by_seq(norm_ch)[:, c, n, :], by_seq(mix_r[:])[:, c, n, :],
                            carry_q[:, c, n, :], ALU.mult, ALU.add))
                chain.wait(t)
                dve_q.add(dve.tensor_copy(carry_q[:], seq[:, :, :, SEG:SEG + 1]))

            def denominator(t):
                act_exp.wait(dve, t)
                chain.done(dve.scalar_tensor_tensor(k_sb[:], mix_k[:], WKV_EPS, mix_v[:], ALU.add, ALU.add), t)
                chain.done(dve.scalar_tensor_tensor(r_sb[:], r_sb[:], 1.0, k_sb[:], ALU.add, ALU.mult), t)

            def invert(t, c):
                chain.link(dve.reciprocal(k_sb[:, c, :], r_sb[:, c, :]))

            def weigh(t):
                pool_num.wait(dve, t)
                chain.wait(t)
                dve_y.add(dve.tensor_tensor(v_sb[:], mix_r[:], k_sb[:], ALU.mult))

            def residual(t):
                pool_x1.wait(dve, t - 1)
                for j in range(2):
                    pe_wo.wait(dve, t, j + 1)
                    dve_x1.add(dve.tensor_tensor(x1_next[:, 2 * j:2 * j + 2, :], A[j][:].rearrange("p (b d) -> p b d", b=2),
                                                 x_in[:, 2 * j:2 * j + 2, :], ALU.add))

            def ln2_statistics(t):
                dve_x1.wait(dve, t)
                statistics(t, x1_next, dve_seed2)

            def ln2(t):
                normalise(t, x1_next, pool_rs2, dve_norm2)

            def rest_x2(t):
                for c in range(DC):
                    act_x2.wait(dve, t, c + 1)
                    dve_x2.add(dve.tensor_tensor(x2_lo[:, c, :], A[2 + c][:], x2_hi[:, c, :].bitcast(F32), ALU.subtract))

            def prod(i, m):
                act_silu.wait(dve, i, m + 1)
                pe_b.wait(dve, i, m + 1)
                b = PAIRS[m % 4][1]
                dve_prod.add(dve.scalar_tensor_tensor(b[:], b[:], s2[:, m:m + 1], mix_k[:, m % 2, :], ALU.mult, ALU.mult))

            def lo(i, m):
                act_hi.wait(dve, i, m + 1)
                dve_lo.add(dve.tensor_tensor(ha_lo[:, m, :], PAIRS[m % 4][1][:], ha_hi[:, m, :].bitcast(F32), ALU.subtract))

            def lo1(i, m):
                act_h1.wait(dve, i, m + 1)
                dve_lo1.add(dve.tensor_tensor(hb_lo[:, m, :], F[m % 4][:], hb_hi[:, m, :].bitcast(F32), ALU.subtract))

            def lo2(i, m):
                act_h2.wait(dve, i, m + 1)
                dve_lo2.add(dve.tensor_tensor(ha_lo[:, m, :], F[m % 4][:], ha_hi[:, m, :].bitcast(F32), ALU.subtract))

            def finish(i):
                st_out.wait(dve, i - 1)
                for j in range(2):
                    pe_w3.wait(dve, i, j + 1)
                    dve_fin.add(dve.tensor_tensor(out_tok[:, 2 * j:2 * j + 2, :], F[j][:].rearrange("p (b d) -> p b d", b=2),
                                                  s3_row[:].rearrange("p (a d) -> p a d", a=1).broadcast_to([P, 2, D]), ALU.mult))

            dve.memset(ones[:], 1.0).then_inc(setup_dve, 1)
            ln1_statistics(0)
            ln1(0)
            dve.wait_ge(ld_const, 16 * 3)
            dve.wait_ge(setup_pool, 2)
            mix(0)
            running_max(0)
            exponents(0)
            recurrence(0)
            denominator(0)
            for c in range(DC):
                invert(0, c)
            weigh(0)
            residual(0)
            ln2_statistics(0)
            dve.wait_ge(flag_sum, 1)
            dve.tensor_reduce(low_max[:], F[0][0:1, 0:5], AX_X, ALU.max).then_inc(flag_max, 1)
            dve.wait_ge(flag_max, 1)
            dve.tensor_scalar(general[:], low_max[:], 1.0, None, ALU.min).then_inc(flag_set, 1)
            dve.wait_ge(flag_set, 1)
            flag = dve.value_load(general[0:1, 0:1], min_val=0, max_val=1)
            with dve.If(flag == 0):
                dve.tensor_copy(w_rnd[:, 0:2 * W12], w_raw[:, 0:2 * W12]).then_inc(rounded_12, 1)
            ln2(0)
            rest_x2(0)
            chain.end_tile()
            with dve.If(flag == 0):
                a = 2 * W12 + HH
                dve.tensor_copy(w_rnd[:, a:a + HH], w_raw[:, a:a + HH]).then_inc(rounded_h2_3, 1)
                dve.tensor_copy(w_rnd[:, a + HH:], w_raw[:, a + HH:]).then_inc(rounded_h2_3, 1)

            def gate(i):
                prod(i, 0)
                for m in range(1, HC - 2):
                    prod(i, m)
                    lo(i, m - 1)
                lo(i, HC - 3)
                for m in range(HC - 2, HC):
                    prod(i, m)
                for m in range(HC - 2, HC):
                    lo(i, m)

            with dve.Fori(0, NT - 1) as i:
                t = i + 1
                gate(i)
                ln1_statistics(t)
                lo1(i, 0)
                ln1(t)
                lo1(i, 1)
                lo1(i, 2)
                mix(t)
                lo1(i, 3)
                lo1(i, 4)
                running_max(t)
                exponents(t)
                recurrence(t)
                lo1(i, 5)
                denominator(t)
                for m in range(6, HC):
                    lo1(i, m)
                invert(t, 0)
                invert(t, 1)
                weigh(t)
                for m in range(5):
                    lo2(i, m)
                residual(t)
                ln2_statistics(t)
                lo2(i, 5)
                ln2(t)
                for m in range(6, HC):
                    lo2(i, m)
                rest_x2(t)
                finish(i)
                chain.end_tile()
            i = NT - 1
            gate(i)
            for m in range(HC):
                lo1(i, m)
            for m in range(HC):
                lo2(i, m)
            finish(i)

        @block.gpsimd
        def _(pool):
            for t in (pool_rs1, pool_rs2, pool_num, pool_out, pool_x1):
                t.start(pool)
            chain = Chain(ctx, nc, "pool_chain", pool, 2 * (4 * NEWTON_STEPS - 1) + 2)

            def refine(t, seed, done):
                seed.wait(pool, t)
                for step in range(NEWTON_STEPS):
                    chain.done(pool.tensor_tensor(newton[:, 0, :], rstd[:], rstd[:], ALU.mult), t)
                    chain.link(pool.tensor_tensor(newton[:, 1, :], newton[:, 0, :], var[:], ALU.mult))
                    chain.wait(t)
                    stand_alone(pool, spare)
                    chain.done(pool.tensor_scalar(newton[:, 0, :], newton[:, 1, :], -0.5, 1.5, ALU.mult, ALU.add), t)
                    y = pool.tensor_tensor(rstd[:], rstd[:], newton[:, 0, :], ALU.mult)
                    if step < NEWTON_STEPS - 1:
                        chain.done(y, t)
                    else:
                        done.add(y)

            def numerator(t):
                act_exp.wait(pool, t, 4)
                dve_q.wait(pool, t)
                chain.link(pool.tensor_tensor(v_sb[:], mix_v[:], v_sb[:], ALU.mult))
                chain.done(pool.tensor_tensor(by_seq(norm_ch), by_seq(mix_k[:]), before, ALU.mult), t)
                pool_num.add(pool.tensor_tensor(mix_r[:], v_sb[:], norm_ch, ALU.add))

            def add_x1(i):
                pool_x1.wait(pool, i)
                for j in range(2):
                    dve_fin.wait(pool, i, j + 1)
                    o = out_tok[:, 2 * j:2 * j + 2, :]
                    pool_out.add(pool.tensor_tensor(o, o, x1[:, 2 * j:2 * j + 2, :], ALU.add))

            def keep_x1(t):
                dve_x1.wait(pool, t)
                pool_out.wait(pool, t - 1)
                stand_alone(pool, spare)
                pool_x1.add(pool.tensor_copy(x1[:], x1_next[:]))

            pool.memset(ident[:], 0.0).then_inc(setup_ident, 1)
            pool.wait_ge(setup_ident, 1)
            pool.affine_select(out=ident[:], in_=ident[:], compare_op=ALU.not_equal, fill=1.0, base=0,
                               pattern=[[-1, P]], channel_multiplier=1).then_inc(setup_pool, 1)
            pool.memset(carry_x[:], 0.0)
            pool.memset(carry_q[:], 0.0)
            pool.memset(carry_p[:], LOWEST).then_inc(setup_pool, 1)
            refine(0, dve_seed1, pool_rs1)
            numerator(0)
            refine(0, dve_seed2, pool_rs2)
            keep_x1(0)
            chain.end_tile()
            with pool.Fori(0, NT - 1) as i:
                refine(i + 1, dve_seed1, pool_rs1)
                numerator(i + 1)
                refine(i + 1, dve_seed2, pool_rs2)
                add_x1(i)
                keep_x1(i + 1)
                chain.end_tile()
            add_x1(NT - 1)


_ORDER = ("x", "vectors", "w_mix", "w_ffn", "s3")


def kernel(**inputs):
    import concourse.bacc as bacc
    from concourse.bass_utils import run_bass_kernel_spmd

    a = {k.removeprefix("L0_"): np.asarray(v) for k, v in inputs.items()}

    def columns(v):
        return v.reshape(-1, P).T

    def by_input(w):
        return w.T.reshape(-1, P, w.shape[0]).transpose(1, 0, 2)

    arrays = {
        "x": a["attn_x"],
        "vectors": np.concatenate([columns(a[k]) for k in (
            "attn_time_mix_k", "attn_time_mix_v", "attn_time_mix_r", "attn_time_decay", "attn_time_first",
            "ffn_w1_s", "ffn_w2_s", "ffn_h1_s", "ffn_h2_s")], axis=1),
        "w_mix": np.stack([by_input(a[f"attn_W_{k}"]) for k in "kvro"], axis=1),
        "w_ffn": np.concatenate([by_input(a[f"ffn_{k}_w"]).reshape(P, -1) for k in ("w1", "w2", "h1", "h2", "w3")], axis=1),
        "s3": a["ffn_w3_s"].reshape(1, -1),
    }
    arrays = {f"in_{k}": np.ascontiguousarray(v) for k, v in arrays.items()}
    nc = bacc.Bacc("TRN2", target_bir_lowering=False, num_devices=1)
    args = [nc.dram_tensor(f"in_{k}", arrays[f"in_{k}"].shape, F32, kind="ExternalInput").ap() for k in _ORDER]
    args.append(nc.dram_tensor("out", a["attn_x"].shape, F32, kind="ExternalOutput").ap())
    build(nc, *args)
    r = run_bass_kernel_spmd(nc, [arrays], core_ids=[0])
    return r.results[0]["out"]
```

```python
from contextlib import ExitStack

import numpy as np

from concourse import mybir

F32 = mybir.dt.float32
F32R = mybir.dt.float32r
BF16 = mybir.dt.bfloat16
U16 = mybir.dt.uint16
I32 = mybir.dt.int32
ALU = mybir.AluOpType
ACT = mybir.ActivationFunctionType
AX_X = mybir.AxisListType.X

P = 128
LN_EPS = 1e-5
WKV_EPS = 1e-9
CLAMP = 30.0
LOWEST = float(np.finfo(np.float32).min)
RSQRT_SEED = 0x5F3759DF
NEWTON_STEPS = 3
WARM = dict(norm1=20, mix=1, y0=14, y1=2, check=2, norm2=2, x2=1)


def stand_alone(eng, spare, tile):
    if not isinstance(tile, int):
        eng.sem_inc(spare, 1)


class Tally:

    def __init__(self, ctx, nc, name, per, unit=1, ahead=1):
        self.sem = ctx.enter_context(nc.semaphore(name))
        self.per, self.unit, self.ahead = per, unit, ahead

    def start(self, eng):
        eng.sem_inc(self.sem, self.per * self.unit)

    def wait(self, eng, tile, k=None):
        k = self.per if k is None else k
        eng.wait_ge(self.sem, tile * (self.per * self.unit) + (self.ahead * self.per + k) * self.unit)

    def add(self, instruction):
        instruction.then_inc(self.sem, self.unit)
        return instruction


class Chain:

    def __init__(self, ctx, nc, name, per=0):
        self.sem = ctx.enter_context(nc.semaphore(name))
        self.per, self.n = per, 0

    def link(self, instruction):
        instruction.then_inc(self.sem, 1)
        self.n += 1

    def wait(self, eng, tile):
        eng.wait_ge(self.sem, tile * self.per + self.n)

    def end_tile(self):
        assert self.n == self.per, (self.n, self.per)
        self.n = 0


class Mixing:

    def __init__(self, ctx, nc, prefix, chunks, seqs, halves, seg, banks, tok, dve_chain, pool_chain, ahead):
        n_seqs, blocks = len(seqs), len(seqs) * halves
        self.seqs = slice(seqs[0], seqs[-1] + 1)
        self.pairs = seqs
        self.blocks = range(seqs[0] * halves, (seqs[-1] + 1) * halves)
        self.cols = slice(seqs[0] * seg, (seqs[-1] + 1) * seg)
        self.banks, self.tok = banks, tok
        self.dve_chain, self.pool_chain = dve_chain, pool_chain

        def tally(name, per):
            return Tally(ctx, nc, prefix + name, per, 1, ahead)

        self.pe_xT = tally("pe_xT", chunks)
        self.pe_kvr = tally("pe_kvr", 3 * chunks)
        self.pe_wo = tally("pe_wo", n_seqs)
        self.pe_x2T = tally("pe_x2T", chunks)
        self.act_x = tally("act_x", 2 + chunks)
        self.act_kvr = tally("act_kvr", 3 * chunks)
        self.act_exp = tally("act_exp", 5)
        self.act_x2 = tally("act_x2", chunks)
        self.dve_norm1 = tally("dve_norm1", blocks)
        self.dve_norm2 = tally("dve_norm2", blocks)
        self.dve_mix = tally("dve_mix", 3 * chunks)
        self.dve_pre = tally("dve_pre", 4)
        self.dve_q = tally("dve_q", 1)
        self.dve_y = tally("dve_y", 1)
        self.dve_x1 = tally("dve_x1", n_seqs)
        self.dve_x2 = tally("dve_x2", chunks)
        self.pool_num = tally("pool_num", 1)
        self.pool_x1 = tally("pool_x1", 1)
        self.of_pe = [self.pe_xT, self.pe_kvr, self.pe_wo, self.pe_x2T]
        self.of_act = [self.act_x, self.act_kvr, self.act_exp, self.act_x2]
        self.of_dve = [self.dve_norm1, self.dve_norm2, self.dve_mix, self.dve_pre, self.dve_q, self.dve_y,
                       self.dve_x1, self.dve_x2]
        self.of_pool = [self.pool_num, self.pool_x1]


def build(nc, x, vectors, w_mix, w_ffn, s3, out):
    n_seq, T, D = x.shape
    DC = D // P
    H = 1024
    HC = H // P
    TILE = 512
    SEG = TILE // n_seq
    HALVES = SEG // P
    NB = TILE // P
    NT = T // SEG
    W12, HH, W3 = DC * H, HC * H, HC * D
    NW = 2 * W12 + 2 * HH + W3
    PIECE = W12
    PIECES = NW // PIECE
    assert vectors.shape[1] == 5 * DC + 4 * HC and w_ffn.shape[1] == NW and NW % PIECE == 0
    assert n_seq == 2 and HALVES == 2

    x_tiles = x.rearrange("n (i h p) d -> n i p h d", h=HALVES, p=P)
    out_tiles = out.rearrange("n (i h p) d -> n i p h d", h=HALVES, p=P)

    with ExitStack() as ctx:
        def sb(name, shape, dt=F32):
            return ctx.enter_context(nc.sbuf_tensor(name, shape, dt))

        def overlay(name, shape, dt):
            with nc.sbuf_tensor(name, shape, dt) as t:
                return t

        def tally(name, per, unit=1):
            return Tally(ctx, nc, name, per, unit)

        w_raw = overlay("w_raw", [P, NW], F32)
        w_rnd = sb("w_rnd", [P, NW], F32R)
        wm = sb("wm", [P, 4, DC, D])
        x_in = sb("x_in", [P, NB, D])
        norm = sb("norm", [P, NB * D])
        seq = sb("seq", [P, DC, n_seq, SEG + 1])
        mix_k = sb("mix_k", [P, DC, TILE])
        mix_v = sb("mix_v", [P, DC, TILE])
        mix_r = sb("mix_r", [P, DC, TILE])
        x2_hi = overlay("x2_hi", [P, DC, TILE], F32R)
        k_sb = sb("k_sb", [P, DC, TILE])
        x2_lo = overlay("x2_lo", [P, DC, TILE], F32R)
        r_sb = sb("r_sb", [P, DC, TILE])
        v_sb = sb("v_sb", [P, DC, TILE])
        x1_next = sb("x1_next", [P, NB, D])
        x1 = sb("x1", [P, NB, D])
        norm_first = overlay("norm_first", [P, NB * D], F32)
        ha_hi = sb("ha_hi", [P, HC, TILE], F32R)
        ha_lo = sb("ha_lo", [P, HC, TILE], F32R)
        unused = overlay("unused", [P, PIECE], BF16)
        hb_hi = sb("hb_hi", [P, HC, TILE], F32R)
        hb_lo = sb("hb_lo", [P, HC, TILE], F32R)
        vec = sb("vec", [P, vectors.shape[1]])
        s3_row = sb("s3_row", [P, D])
        ident = sb("ident", [P, P])
        carry_x = sb("carry_x", [P, DC, n_seq, 1])
        carry_p = sb("carry_p", [P, DC, n_seq, 1])
        carry_q = sb("carry_q", [P, DC, n_seq, 1])
        stats = sb("stats", [P, NB, 6])
        moments = sb("moments", [P, NB, 2])
        var = sb("var", [P, NB])
        shifted = sb("shifted", [P, NB], I32)
        rstd = sb("rstd", [P, NB])
        newton = sb("newton", [P, NB])
        low_sums = sb("low_sums", [P, PIECES])
        low_max = sb("low_max", [1, 1])
        ones = sb("ones", [P, 1])
        general = sb("general", [1, 1], I32)

        F = [ctx.enter_context(nc.psum_tensor(f"ffn{i}", [P, 512], F32)) for i in range(4)]
        A = [ctx.enter_context(nc.psum_tensor(f"att{i}", [P, 512], F32)) for i in range(4)]
        PAIRS = [(F[2], F[3]), (F[0], F[1]), (A[0], A[1]), (A[2], A[3])]
        KVR_BANK = [2, 3, 0, 1, 2, 3]

        tmk, tmv, tmr, decay, first = (vec[:, DC * j:DC * (j + 1)] for j in range(5))
        s1, s2, sh1, sh2 = (vec[:, 5 * DC + HC * j:5 * DC + HC * (j + 1)] for j in range(4))
        norm_ch = norm[:].rearrange("p (c t) -> p c t", c=DC)

        def by_seq(ap):
            return ap.rearrange("p c (n t) -> p c n t", n=n_seq)

        def by_block(ap):
            return ap.rearrange("p (b d) -> p b d", b=NB)

        out_tok = by_block(mix_v[:].rearrange("p c t -> p (c t)"))
        now, before = seq[:, :, :, 1:], seq[:, :, :, 0:SEG]

        def ffn_weights(w):
            a = 0
            parts = []
            for n, c in ((W12, DC), (W12, DC), (HH, HC), (HH, HC), (W3, HC)):
                parts.append(w[:, a:a + n].rearrange("p (c o) -> p c o", c=c))
                a += n
            return parts

        def semaphore(name):
            return ctx.enter_context(nc.semaphore(name))

        LOADS = [W12, W12, HH // 2, HH // 2, HH // 2, HH // 2, W3]
        ld_const = semaphore("ld_const")
        ld_first = [semaphore(f"ld_first{n}") for n in range(n_seq)]
        ld_w = [semaphore(f"ld_w{k}") for k in range(len(LOADS))]
        setup_ident = semaphore("setup_ident")
        setup_pool = semaphore("setup_pool")
        setup_dve = semaphore("setup_dve")
        low_done = semaphore("low_done")
        flag_sum = semaphore("flag_sum")
        flag_max = semaphore("flag_max")
        flag_set = semaphore("flag_set")
        spare = semaphore("spare")
        rounded_w1, rounded_w2, rounded_h1, rounded_h2, rounded_w3 = (
            semaphore("rounded_" + w) for w in ("w1", "w2", "h1", "h2", "w3"))
        W1_AT, W2_AT, H1_AT, H2_AT, W3_AT = 0, W12, 2 * W12, 2 * W12 + HH, 2 * W12 + 2 * HH
        H1_SHARE = W12

        def rounded(copy, a, n):
            return copy(w_rnd[:, a:a + n], w_raw[:, a:a + n])

        first_chains = Chain(ctx, nc, "first_dve_chain"), Chain(ctx, nc, "first_pool_chain")
        FIRST = [Mixing(ctx, nc, f"first{n}_", DC, range(n, n + 1), HALVES, SEG, (A, F)[n], by_block(norm_first[:]),
                        *first_chains, ahead=0) for n in range(n_seq)]
        WHOLE = Mixing(ctx, nc, "", DC, range(n_seq), HALVES, SEG, A, by_block(norm[:]),
                       Chain(ctx, nc, "dve_chain", 61), Chain(ctx, nc, "pool_chain", 2), ahead=1)

        def hand_over(eng, firsts, wholes, chain=None):
            for *parts, whole in reversed(list(zip(*firsts, wholes))):
                for part in parts:
                    part.wait(eng, 0)
                eng.sem_inc(whole.sem, 2 * whole.per)
            if chain:
                eng.sem_inc(chain.sem, chain.per)

        pe_a, pe_b, pe_h1, pe_h2 = (tally(n, HC) for n in ("pe_a", "pe_b", "pe_h1", "pe_h2"))
        pe_w3 = tally("pe_w3", 2)
        act_silu, act_hi = tally("act_silu", HC), tally("act_hi", HC)
        act_hi1, act_h1, act_hi2, act_h2 = (tally(n, HC) for n in ("act_hi1", "act_h1", "act_hi2", "act_h2"))
        dve_prod, dve_lo, dve_lo1, dve_lo2 = (tally(n, HC) for n in ("dve_prod", "dve_lo", "dve_lo1", "dve_lo2"))
        dve_fin = tally("dve_fin", 2)
        pool_out = tally("pool_out", 2)
        ld_x = tally("ld_x", n_seq, 16)
        st_out = tally("st_out", n_seq, 16)

        block = ctx.enter_context(nc.Block())

        @block.sync
        def _(sp):
            st_out.start(sp)

            def load_x(t):
                WHOLE.dve_x1.wait(sp, t - 1)
                for n in range(n_seq):
                    ld_x.add(sp.dma_start(x_in[:, HALVES * n:HALVES * (n + 1), :], x_tiles[n, t]))

            def store(i):
                for j in range(2):
                    pool_out.wait(sp, i, j + 1)
                    st_out.add(sp.dma_start(out_tiles[j, i], out_tok[:, HALVES * j:HALVES * (j + 1), :]))

            for n in range(n_seq):
                sp.dma_start(x_in[:, HALVES * n:HALVES * (n + 1), :], x_tiles[n, 0]).then_inc(ld_first[n], 16)
            sp.dma_start(vec[:], vectors).then_inc(ld_const, 16)
            sp.dma_start(wm[:], w_mix).then_inc(ld_const, 16)
            sp.dma_start(s3_row[:], s3.broadcast_to([P, D])).then_inc(ld_const, 16)
            a = 0
            for n, loaded in zip(LOADS, ld_w):
                sp.dma_start(w_raw[:, a:a + n], w_ffn[:, a:a + n]).then_inc(loaded, 16)
                a += n
            for n in range(n_seq):
                sp.wait_ge(ld_first[n], 16)
            sp.sem_inc(ld_x.sem, 2 * 16 * n_seq)
            with sp.Fori(0, NT - 1) as i:
                load_x(i + 1)
                store(i)
            store(NT - 1)
            st_out.wait(sp, NT - 1)

        @block.tensor
        def _(pe):
            for t in (pe_a, pe_b, pe_h1, pe_h2, pe_w3):
                t.start(pe)

            def keep_warm(n, moving, bank=F[3]):
                bank = bank[:, 0:moving.free_size()]
                for _ in range(n):
                    pe.matmul(bank, ident[:], moving, start=True, stop=True)

            def transposed(s, bank, b, c):
                return pe.transpose(bank[:, b * P:(b + 1) * P], s.tok[:, b, c * P:(c + 1) * P], ident[:])

            def transpose_x(s, t):
                s.dve_norm1.wait(pe, t)
                for c in range(DC):
                    for b in s.blocks:
                        mm = transposed(s, s.banks[c], b, c)
                    s.pe_xT.add(mm)

            def project(s, t, chunks=range(3 * DC)):
                for j in chunks:
                    which, e = divmod(j, DC)
                    src = (mix_k, mix_v, mix_r)[which]
                    s.dve_mix.wait(pe, t, (which + 1) * DC)
                    if j >= 4:
                        s.act_kvr.wait(pe, t, j - 3)
                    for c in range(DC):
                        mm = pe.matmul(s.banks[KVR_BANK[j]][:, s.cols], wm[:, which, c, e * P:(e + 1) * P],
                                       src[:, c, s.cols], start=(c == 0), stop=(c == DC - 1))
                    s.pe_kvr.add(mm)

            def project_out(s, t):
                s.dve_y.wait(pe, t)
                for b in s.blocks:
                    for c in range(DC):
                        mm = pe.matmul(s.banks[b // 2][:, (b % 2) * D:(b % 2 + 1) * D], v_sb[:, c, b * P:(b + 1) * P],
                                       wm[:, 3, c, :], start=(c == 0), stop=(c == DC - 1))
                    if b % 2:
                        s.pe_wo.add(mm)

            def transpose_x2(s, t):
                s.dve_norm2.wait(pe, t)
                for c in range(DC):
                    for b in s.blocks:
                        mm = transposed(s, s.banks[2 + c], b, c)
                    s.pe_x2T.add(mm)

            def mlp(exact):
                w1, w2, wh1, wh2, w3 = ffn_weights(w_rnd if exact else w_raw)

                def act(ap):
                    return ap if exact else ap.bitcast(F32)

                def gate(i):
                    WHOLE.dve_x2.wait(pe, i)
                    if exact:
                        pe.wait_ge(rounded_w1, 1)
                        pe.wait_ge(rounded_w2, 1)
                    order = [(m, j) for m in range(HC - 2) for j in range(2)]
                    order += [(m, j) for j in range(2) for m in (HC - 2, HC - 1)]
                    for m, j in order:
                        if m == 1 and j == 0:
                            dve_fin.wait(pe, i - 1)
                        if m >= 4 and j == 0:
                            dve_lo.wait(pe, i, m - 3)
                        w, done, bank = (w1, w2)[j], (pe_a, pe_b)[j], PAIRS[m % 4][j]
                        for c in range(DC):
                            w_mc = w[:, c, m * P:(m + 1) * P]
                            pe.matmul(bank[:], w_mc, act(x2_hi[:, c, :]), start=(c == 0), stop=False)
                            mm = pe.matmul(bank[:], w_mc, act(x2_lo[:, c, :]), start=False, stop=(c == DC - 1))
                        done.add(mm)

                EARLY = 6

                def hidden(i, w, hi, lo, hi_ready, ready, before_, evacuated, done, chunks):
                    def accumulate(m, inputs, fresh=False):
                        for c in inputs:
                            if fresh:
                                hi_ready.wait(pe, i, c + 1)
                            w_mc = w[:, c, m * P:(m + 1) * P]
                            pe.matmul(F[m % 4][:], w_mc, act(hi[:, c, :]), start=(c == 0), stop=False)
                            if fresh:
                                ready.wait(pe, i, c + 1)
                            mm = pe.matmul(F[m % 4][:], w_mc, act(lo[:, c, :]), start=False, stop=(c == HC - 1))
                        if inputs[-1] == HC - 1:
                            done.add(mm)

                    for m in chunks:
                        if m < 4:
                            tally_, k = before_(m)
                            tally_.wait(pe, i, k)
                        else:
                            evacuated.wait(pe, i, m - 3)
                        if m == 0:
                            ready.wait(pe, i, EARLY - 1)
                            accumulate(0, range(EARLY - 1))
                            ready.wait(pe, i, EARLY)
                            accumulate(0, range(EARLY - 1, EARLY))
                        elif m == 1:
                            accumulate(1, range(EARLY))
                            accumulate(0, range(EARLY, HC), fresh=True)
                            accumulate(1, range(EARLY, HC))
                        else:
                            accumulate(m, range(HC))

                def hidden1(i, chunks):
                    if exact and 0 in chunks:
                        pe.wait_ge(rounded_h1, 2)
                    hidden(i, wh1, ha_hi, ha_lo, act_hi, dve_lo, lambda m: (dve_lo, 6), dve_lo1, pe_h1, chunks)

                def hidden2(i, chunks):
                    if exact and 0 in chunks:
                        pe.wait_ge(rounded_h2, 1)
                    hidden(i, wh2, hb_hi, hb_lo, act_hi1, dve_lo1, lambda m: (dve_lo1, m + 5), dve_lo2, pe_h2, chunks)

                def last(i):
                    if exact:
                        pe.wait_ge(rounded_w3, 1)
                    def accumulate(b, inputs, fresh=False):
                        bank = F[b // 2][:, (b % 2) * D:(b % 2 + 1) * D]
                        for c in inputs:
                            if fresh:
                                dve_lo2.wait(pe, i, c + 1)
                            tokens = slice(b * P, (b + 1) * P)
                            pe.matmul(bank, act(ha_hi[:, c, tokens]), w3[:, c, :], start=(c == 0), stop=False)
                            mm = pe.matmul(bank, act(ha_lo[:, c, tokens]), w3[:, c, :], start=False, stop=(c == HC - 1))
                        if b % 2:
                            pe_w3.add(mm)

                    dve_lo2.wait(pe, i, EARLY)
                    accumulate(0, range(EARLY))
                    accumulate(2, range(EARLY))
                    accumulate(0, range(EARLY, HC), fresh=True)
                    accumulate(1, range(HC))
                    accumulate(2, range(EARLY, HC))
                    accumulate(3, range(HC))

                with pe.Fori(0, NT - 1) as i:
                    gate(i)
                    hidden1(i, [0, 1, 2])
                    transpose_x(WHOLE, i + 1)
                    hidden1(i, [3, 4])
                    project(WHOLE, i + 1)
                    hidden1(i, range(5, HC))
                    hidden2(i, range(5))
                    project_out(WHOLE, i + 1)
                    hidden2(i, range(5, HC))
                    transpose_x2(WHOLE, i + 1)
                    last(i)
                i = NT - 1
                gate(i)
                hidden1(i, range(HC))
                hidden2(i, range(HC))
                last(i)

            pe.wait_ge(setup_pool, 1)
            keep_warm(WARM["norm1"], ident[:])
            for s in FIRST:
                transpose_x(s, 0)
            pe.wait_ge(ld_const, 16 * 3)
            w_k = wm[:, 0, :, :].rearrange("p c d -> p (c d)")
            FIRST[-1].act_x.wait(pe, 0)
            keep_warm(WARM["mix"], w_k)
            for s in FIRST:
                project(s, 0, range(DC))
            for s in FIRST:
                project(s, 0, range(DC, 3 * DC))
            FIRST[-1].act_kvr.wait(pe, 0)
            keep_warm(WARM["y0"], w_k)
            for n, s in enumerate(FIRST):
                project_out(s, 0)
                keep_warm(WARM[("y1", "check")[n]], w_k)
            pe.wait_ge(setup_dve, 1)
            pe.wait_ge(low_done, PIECES)
            pe.matmul(F[0][0:1, 0:PIECES], ones[:], low_sums[:], start=True, stop=True).then_inc(flag_sum, 1)
            keep_warm(WARM["norm2"], w_k)
            for s in FIRST:
                transpose_x2(s, 0)
            hand_over(pe, [s.of_pe for s in FIRST], WHOLE.of_pe)
            pe.wait_ge(flag_set, 1)
            keep_warm(WARM["x2"], w_k, F[0])
            flag = pe.value_load(general[0:1, 0:1], min_val=0, max_val=1)
            with pe.If(flag > 0):
                mlp(exact=False)
            with pe.Else():
                mlp(exact=True)

        @block.scalar
        def _(act):
            for t in (act_silu, act_hi, act_hi1, act_h1, act_hi2, act_h2):
                t.start(act)

            def copy_x(s, t):
                if s is WHOLE:
                    s.pool_num.wait(act, t - 1)
                    s.act_x.wait(act, t - 1)
                s.act_x.add(act.activation(seq[:, :, s.seqs, 0:1], carry_x[:, :, s.seqs], ACT.Copy))
                for c in range(DC):
                    s.pe_xT.wait(act, t, c + 1)
                    x_ch = s.banks[c][:].rearrange("p (n t) -> p n t", n=n_seq)
                    s.act_x.add(act.activation(now[:, c, s.seqs], x_ch[:, s.seqs], ACT.Copy))
                s.act_x.wait(act, t, 1 + DC)
                s.act_x.add(act.activation(carry_x[:, :, s.seqs], seq[:, :, s.seqs, SEG:SEG + 1], ACT.Copy))

            def copy_kvr(s, t, chunks=range(3 * DC)):
                for j in chunks:
                    which, e = divmod(j, DC)
                    s.pe_kvr.wait(act, t, j + 1)
                    s.act_kvr.add(act.activation((k_sb, v_sb, r_sb)[which][:, e, s.cols],
                                                 s.banks[KVR_BANK[j]][:, s.cols], ACT.Copy))

            def exps(s, t):
                s.dve_pre.wait(act, t)
                for ap, sign in ((mix_r, -1.0), (norm_ch, 1.0), (mix_v, 1.0), (mix_k, -1.0)):
                    s.act_exp.add(act.activation(ap[:, :, s.cols], ap[:, :, s.cols], ACT.Exp, scale=sign))
                s.act_kvr.wait(act, t)
                s.act_exp.add(act.activation(r_sb[:, :, s.cols], r_sb[:, :, s.cols], ACT.Exp, scale=-1.0))

            def round_x2(s, t):
                for c in range(DC):
                    s.pe_x2T.wait(act, t, c + 1)
                    s.act_x2.add(act.activation(x2_hi[:, c, s.cols], s.banks[2 + c][:, s.cols], ACT.Copy))

            def gate(i):
                def silu(m):
                    pe_a.wait(act, i, m + 1)
                    if m >= 2:
                        dve_prod.wait(act, i, m - 1)
                    act_silu.add(act.activation(mix_k[:, m % 2, :], PAIRS[m % 4][0][:], ACT.Silu, scale=s1[:, m:m + 1]))

                def hi(m):
                    dve_prod.wait(act, i, m + 1)
                    act_hi.add(act.activation(ha_hi[:, m, :], PAIRS[m % 4][1][:], ACT.Copy))

                silu(0)
                for m in range(1, HC):
                    silu(m)
                    hi(m - 1)
                hi(HC - 1)

            def gelu(i, m, scale, ready, hi, hi_done, done):
                ready.wait(act, i, m + 1)
                hi_done.add(act.activation(hi[:, m, :], F[m % 4][:], ACT.Gelu, scale=scale[:, m:m + 1]))
                hi_done.wait(act, i, m + 1)
                done.add(act.activation(F[m % 4][:], F[m % 4][:], ACT.Gelu, scale=scale[:, m:m + 1]))

            def gelu1(i, m):
                gelu(i, m, sh1, pe_h1, hb_hi, act_hi1, act_h1)

            def gelu2(i, m):
                gelu(i, m, sh2, pe_h2, ha_hi, act_hi2, act_h2)

            act.wait_ge(setup_pool, 2)
            halves = w_raw[:].bitcast(U16).rearrange("p (n two) -> p n two", two=2)[:, :, 0]
            ends = np.cumsum(LOADS)

            def act_copy(dst, src):
                return act.activation(dst, src, ACT.Copy)

            def check_piece(k):
                load = int(np.searchsorted(ends, PIECE * k, side="right"))
                act.wait_ge(ld_w[load], 16)
                act.wait_ge(low_done, k)
                act.activation(unused[:], halves[:, PIECE * k:PIECE * (k + 1)], ACT.Copy,
                               accum_out=low_sums[:, k:k + 1]).then_inc(low_done, 1)

            for s in FIRST:
                copy_x(s, 0)
            check_piece(0)
            for n, s in enumerate(FIRST):
                copy_kvr(s, 0, range(DC))
                check_piece(1 + n)
            for s in FIRST:
                copy_kvr(s, 0, range(DC, 3 * DC))
            for s in FIRST:
                exps(s, 0)
            for k in range(3, PIECES):
                check_piece(k)
            act.wait_ge(flag_set, 1)
            flag = act.value_load(general[0:1, 0:1], min_val=0, max_val=1)
            with act.If(flag == 0):
                rounded(act_copy, W2_AT, W12).then_inc(rounded_w2, 1)
            for s in FIRST:
                round_x2(s, 0)
            hand_over(act, [s.of_act for s in FIRST], WHOLE.of_act)
            with act.If(flag == 0):
                rounded(act_copy, H1_AT, H1_SHARE).then_inc(rounded_h1, 1)

            with act.Fori(0, NT - 1) as i:
                gate(i)
                gelu1(i, 0)
                gelu1(i, 1)
                gelu1(i, 2)
                copy_x(WHOLE, i + 1)
                gelu1(i, 3)
                gelu1(i, 4)
                copy_kvr(WHOLE, i + 1)
                exps(WHOLE, i + 1)
                for m in range(5, HC):
                    gelu1(i, m)
                for m in range(HC):
                    gelu2(i, m)
                round_x2(WHOLE, i + 1)
            i = NT - 1
            gate(i)
            for m in range(HC):
                gelu1(i, m)
            for m in range(HC):
                gelu2(i, m)

        @block.vector
        def _(dve):
            for t in (dve_prod, dve_lo, dve_lo1, dve_lo2, dve_fin):
                t.start(dve)

            def link(s, instruction):
                s.dve_chain.link(instruction)

            def settle(s, t):
                s.dve_chain.wait(dve, t)

            def statistics(s, t, src):
                settle(s, t)
                for b in s.blocks:
                    link(s, dve.bn_stats(stats[:, b, :], src[:, b, :]))
                settle(s, t)
                stand_alone(dve, spare, t)
                for b in s.blocks:
                    link(s, dve.bn_aggr(moments[:, b, :], stats[:, b, :]))

            def reciprocal_deviation(s, t, blocks):
                b = slice(blocks[0], blocks[-1] + 1)
                v, y, u = var[:, b], rstd[:, b], newton[:, b]
                settle(s, t)
                link(s, dve.tensor_scalar(v, moments[:, b, 1], LN_EPS, None, ALU.add))
                settle(s, t)
                link(s, dve.tensor_scalar(shifted[:, b], v.bitcast(I32), 1, None, ALU.arith_shift_right))
                settle(s, t)
                link(s, dve.tensor_scalar(y.bitcast(I32), shifted[:, b], -1.0, float(RSQRT_SEED), ALU.mult, ALU.add))
                settle(s, t)
                for _ in range(NEWTON_STEPS):
                    link(s, dve.tensor_tensor(u, y, y, ALU.mult))
                    settle(s, t)
                    link(s, dve.scalar_tensor_tensor(u, u, -0.5, v, ALU.mult, ALU.mult))
                    settle(s, t)
                    link(s, dve.scalar_tensor_tensor(y, u, 1.5, y, ALU.add, ALU.mult))
                    settle(s, t)

            def normalise(s, t, src, done):
                for b in s.blocks:
                    done.add(dve.tensor_scalar(s.tok[:, b, :], src[:, b, :], moments[:, b, 0:1], rstd[:, b:b + 1],
                                               ALU.subtract, ALU.mult))

            def ln1_statistics(s, t):
                statistics(s, t, x_in)

            def ln1(s, t):
                normalise(s, t, x_in, s.dve_norm1)

            def mix(s, t):
                s.act_x.wait(dve, t, 1 + DC)
                if s is WHOLE:
                    st_out.wait(dve, t - 2)
                    dve_prod.wait(dve, t - 1)
                diff = by_seq(norm_ch)[:, :, s.seqs]
                link(s, dve.tensor_tensor(diff, now[:, :, s.seqs], before[:, :, s.seqs], ALU.subtract))
                settle(s, t)
                for dst, tm in ((mix_k, tmk), (mix_v, tmv), (mix_r, tmr)):
                    for c in range(DC):
                        s.dve_mix.add(dve.scalar_tensor_tensor(
                            by_seq(dst[:])[:, c, s.seqs], diff[:, c], tm[:, c:c + 1], before[:, c, s.seqs],
                            ALU.mult, ALU.add))

            def running_max(s, t):
                s.act_kvr.wait(dve, t, DC)
                s.dve_mix.wait(dve, t)
                link(s, dve.tensor_copy(seq[:, :, s.seqs, 0:1], carry_p[:, :, s.seqs]))
                settle(s, t)
                for c in range(DC):
                    for n in s.pairs:
                        link(s, dve.tensor_tensor_scan(
                            now[:, c, n, :], decay[:, c:c + 1].broadcast_to([P, SEG]), by_seq(k_sb[:])[:, c, n, :],
                            carry_p[:, c, n, :], ALU.add, ALU.max))
                settle(s, t)
                link(s, dve.tensor_copy(carry_p[:, :, s.seqs], seq[:, :, s.seqs, SEG:SEG + 1]))

            def exponents(s, t):
                e, g = mix_k[:, :, s.cols], norm_ch[:, :, s.cols]
                e4, g4, k4 = (by_seq(a[:])[:, :, s.seqs] for a in (mix_k, norm_ch, k_sb))
                p4 = before[:, :, s.seqs]
                s.pe_kvr.wait(dve, t, DC)
                for c in range(DC):
                    link(s, dve.scalar_tensor_tensor(e4[:, c], k4[:, c], first[:, c:c + 1], p4[:, c],
                                                     ALU.add, ALU.subtract))
                for c in range(DC):
                    link(s, dve.scalar_tensor_tensor(g4[:, c], p4[:, c], decay[:, c:c + 1], k4[:, c],
                                                     ALU.add, ALU.subtract))
                settle(s, t)
                s.pe_kvr.wait(dve, t, 2 * DC)
                s.dve_pre.add(dve.tensor_scalar(mix_v[:, :, s.cols], e, 0.0, -CLAMP, ALU.min, ALU.max))
                s.dve_pre.wait(dve, t, 1)
                s.dve_pre.add(dve.tensor_scalar(e, e, 0.0, CLAMP, ALU.max, ALU.min))
                s.pe_kvr.wait(dve, t, 3 * DC)
                s.dve_pre.add(dve.tensor_scalar(mix_r[:, :, s.cols], g, 0.0, CLAMP, ALU.max, ALU.min))
                s.dve_pre.wait(dve, t, 3)
                s.dve_pre.add(dve.tensor_scalar(g, g, 0.0, -CLAMP, ALU.min, ALU.max))

            def recurrence(s, t):
                s.act_exp.wait(dve, t, 2)
                new = mix_r[:, :, s.cols]
                link(s, dve.tensor_tensor(new, new, v_sb[:, :, s.cols], ALU.mult))
                settle(s, t)
                link(s, dve.tensor_copy(seq[:, :, s.seqs, 0:1], carry_q[:, :, s.seqs]))
                for c in range(DC):
                    for n in s.pairs:
                        link(s, dve.tensor_tensor_scan(
                            now[:, c, n, :], by_seq(norm_ch)[:, c, n, :], by_seq(mix_r[:])[:, c, n, :],
                            carry_q[:, c, n, :], ALU.mult, ALU.add))
                settle(s, t)
                s.dve_q.add(dve.tensor_copy(carry_q[:, :, s.seqs], seq[:, :, s.seqs, SEG:SEG + 1]))

            def denominator(s, t):
                s.act_exp.wait(dve, t)
                k_, r_ = k_sb[:, :, s.cols], r_sb[:, :, s.cols]
                scale_old, scale_cur = mix_k[:, :, s.cols], mix_v[:, :, s.cols]
                link(s, dve.scalar_tensor_tensor(k_, scale_old, WKV_EPS, scale_cur, ALU.add, ALU.add))
                settle(s, t)
                link(s, dve.scalar_tensor_tensor(r_, r_, 1.0, k_, ALU.add, ALU.mult))
                settle(s, t)

            def invert(s, t):
                for c in range(DC):
                    link(s, dve.reciprocal(k_sb[:, c, s.cols], r_sb[:, c, s.cols]))

            def weigh(s, t):
                s.pool_num.wait(dve, t)
                settle(s, t)
                s.dve_y.add(dve.tensor_tensor(v_sb[:, :, s.cols], mix_r[:, :, s.cols], k_sb[:, :, s.cols], ALU.mult))

            def residual(s, t):
                if s is WHOLE:
                    s.pool_x1.wait(dve, t - 1)
                for k, j in enumerate(s.pairs):
                    s.pe_wo.wait(dve, t, k + 1)
                    pair = slice(2 * j, 2 * j + 2)
                    mixed = s.banks[j][:].rearrange("p (b d) -> p b d", b=2)
                    s.dve_x1.add(dve.tensor_tensor(x1_next[:, pair, :], mixed, x_in[:, pair, :], ALU.add))

            def ln2_statistics(s, t):
                s.dve_x1.wait(dve, t)
                statistics(s, t, x1_next)

            def ln2(s, t):
                normalise(s, t, x1_next, s.dve_norm2)

            def rest_x2(s, t):
                for c in range(DC):
                    s.act_x2.wait(dve, t, c + 1)
                    s.dve_x2.add(dve.tensor_tensor(x2_lo[:, c, s.cols], s.banks[2 + c][:, s.cols],
                                                   x2_hi[:, c, s.cols].bitcast(F32), ALU.subtract))

            def prod(i, m):
                act_silu.wait(dve, i, m + 1)
                pe_b.wait(dve, i, m + 1)
                b = PAIRS[m % 4][1]
                dve_prod.add(dve.scalar_tensor_tensor(b[:], b[:], s2[:, m:m + 1], mix_k[:, m % 2, :],
                                                      ALU.mult, ALU.mult))

            def lo(i, m):
                act_hi.wait(dve, i, m + 1)
                dve_lo.add(dve.tensor_tensor(ha_lo[:, m, :], PAIRS[m % 4][1][:], ha_hi[:, m, :].bitcast(F32),
                                             ALU.subtract))

            def lo1(i, m):
                act_h1.wait(dve, i, m + 1)
                dve_lo1.add(dve.tensor_tensor(hb_lo[:, m, :], F[m % 4][:], hb_hi[:, m, :].bitcast(F32), ALU.subtract))

            def lo2(i, m):
                act_h2.wait(dve, i, m + 1)
                dve_lo2.add(dve.tensor_tensor(ha_lo[:, m, :], F[m % 4][:], ha_hi[:, m, :].bitcast(F32), ALU.subtract))

            def finish(i):
                st_out.wait(dve, i - 1)
                s3_pair = s3_row[:].rearrange("p (a d) -> p a d", a=1).broadcast_to([P, 2, D])
                for j in range(2):
                    pe_w3.wait(dve, i, j + 1)
                    result = F[j][:].rearrange("p (b d) -> p b d", b=2)
                    dve_fin.add(dve.tensor_tensor(out_tok[:, 2 * j:2 * j + 2, :], result, s3_pair, ALU.mult))

            dve.memset(ones[:], 1.0).then_inc(setup_dve, 1)
            for n, s in enumerate(FIRST):
                dve.wait_ge(ld_first[n], 16)
                ln1_statistics(s, 0)
            reciprocal_deviation(FIRST[-1], 0, range(NB))
            for s in FIRST:
                ln1(s, 0)
            dve.wait_ge(ld_const, 16 * 3)
            dve.wait_ge(setup_pool, 2)
            for s in FIRST:
                mix(s, 0)
            for s in FIRST:
                running_max(s, 0)
                exponents(s, 0)
            for s in FIRST:
                recurrence(s, 0)
            denominator(FIRST[0], 0)
            invert(FIRST[0], 0)
            denominator(FIRST[1], 0)
            weigh(FIRST[0], 0)
            invert(FIRST[1], 0)
            weigh(FIRST[1], 0)
            for s in FIRST:
                residual(s, 0)
                ln2_statistics(s, 0)
            reciprocal_deviation(FIRST[-1], 0, range(NB))
            dve.wait_ge(flag_sum, 1)
            dve.tensor_reduce(low_max[:], F[0][0:1, 0:PIECES], AX_X, ALU.max).then_inc(flag_max, 1)
            dve.wait_ge(flag_max, 1)
            dve.tensor_scalar(general[:], low_max[:], 1.0, None, ALU.min).then_inc(flag_set, 1)
            for s in FIRST:
                ln2(s, 0)
            dve.wait_ge(flag_set, 1)
            flag = dve.value_load(general[0:1, 0:1], min_val=0, max_val=1)
            with dve.If(flag == 0):
                rounded(dve.tensor_copy, W1_AT, W12).then_inc(rounded_w1, 1)
            for s in FIRST:
                rest_x2(s, 0)
            hand_over(dve, [s.of_dve for s in FIRST], WHOLE.of_dve, WHOLE.dve_chain)
            with dve.If(flag == 0):
                rounded(dve.tensor_copy, H1_AT + H1_SHARE, HH - H1_SHARE).then_inc(rounded_h1, 1)

            def gate(i):
                prod(i, 0)
                for m in range(1, HC - 2):
                    prod(i, m)
                    lo(i, m - 1)
                lo(i, HC - 3)
                for m in range(HC - 2, HC):
                    prod(i, m)
                for m in range(HC - 2, HC):
                    lo(i, m)

            with dve.Fori(0, NT - 1) as i:
                t = i + 1
                gate(i)
                ld_x.wait(dve, t)
                ln1_statistics(WHOLE, t)
                reciprocal_deviation(WHOLE, t, WHOLE.blocks)
                ln1(WHOLE, t)
                lo1(i, 0)
                lo1(i, 1)
                lo1(i, 2)
                mix(WHOLE, t)
                lo1(i, 3)
                lo1(i, 4)
                running_max(WHOLE, t)
                exponents(WHOLE, t)
                recurrence(WHOLE, t)
                lo1(i, 5)
                denominator(WHOLE, t)
                for m in range(6, HC):
                    lo1(i, m)
                invert(WHOLE, t)
                weigh(WHOLE, t)
                for m in range(5):
                    lo2(i, m)
                residual(WHOLE, t)
                ln2_statistics(WHOLE, t)
                lo2(i, 5)
                reciprocal_deviation(WHOLE, t, WHOLE.blocks)
                ln2(WHOLE, t)
                for m in range(6, HC):
                    lo2(i, m)
                rest_x2(WHOLE, t)
                finish(i)
                WHOLE.dve_chain.end_tile()
            i = NT - 1
            gate(i)
            for m in range(HC):
                lo1(i, m)
            for m in range(HC):
                lo2(i, m)
            finish(i)

        @block.gpsimd
        def _(pool):
            pool_out.start(pool)

            def settle(s, t):
                s.pool_chain.wait(pool, t)

            def numerator(s, t):
                s.act_exp.wait(pool, t, 4)
                s.dve_q.wait(pool, t)
                v_, old_q = v_sb[:, :, s.cols], by_seq(norm_ch)[:, :, s.seqs]
                s.pool_chain.link(pool.tensor_tensor(v_, mix_v[:, :, s.cols], v_, ALU.mult))
                scale_old = by_seq(mix_k[:])[:, :, s.seqs]
                s.pool_chain.link(pool.tensor_tensor(old_q, scale_old, before[:, :, s.seqs], ALU.mult))
                settle(s, t)
                s.pool_num.add(pool.tensor_tensor(mix_r[:, :, s.cols], v_, norm_ch[:, :, s.cols], ALU.add))

            def add_x1(i):
                WHOLE.pool_x1.wait(pool, i)
                for j in range(2):
                    dve_fin.wait(pool, i, j + 1)
                    o = out_tok[:, 2 * j:2 * j + 2, :]
                    pool_out.add(pool.tensor_tensor(o, o, x1[:, 2 * j:2 * j + 2, :], ALU.add))

            def keep_x1(s, t):
                s.dve_x1.wait(pool, t)
                if s is WHOLE:
                    pool_out.wait(pool, t - 1)
                    stand_alone(pool, spare, t)
                b = slice(s.blocks[0], s.blocks[-1] + 1)
                s.pool_x1.add(pool.tensor_copy(x1[:, b, :], x1_next[:, b, :]))

            pool.memset(ident[:], 0.0).then_inc(setup_ident, 1)
            pool.wait_ge(setup_ident, 1)
            pool.affine_select(out=ident[:], in_=ident[:], compare_op=ALU.not_equal, fill=1.0, base=0,
                               pattern=[[-1, P]], channel_multiplier=1).then_inc(setup_pool, 1)
            pool.memset(carry_x[:], 0.0)
            pool.memset(carry_q[:], 0.0)
            pool.memset(carry_p[:], LOWEST).then_inc(setup_pool, 1)
            for s in FIRST:
                numerator(s, 0)
            for s in FIRST:
                keep_x1(s, 0)
            hand_over(pool, [s.of_pool for s in FIRST], WHOLE.of_pool, WHOLE.pool_chain)
            pool.wait_ge(flag_set, 1)
            flag = pool.value_load(general[0:1, 0:1], min_val=0, max_val=1)
            with pool.If(flag == 0):
                rounded(pool.tensor_copy, H2_AT, HH).then_inc(rounded_h2, 1)
                rounded(pool.tensor_copy, W3_AT, W3).then_inc(rounded_w3, 1)
            with pool.Fori(0, NT - 1) as i:
                numerator(WHOLE, i + 1)
                add_x1(i)
                keep_x1(WHOLE, i + 1)
                WHOLE.pool_chain.end_tile()
            add_x1(NT - 1)


_ORDER = ("x", "vectors", "w_mix", "w_ffn", "s3")


def kernel(**inputs):
    import concourse.bacc as bacc
    from concourse.bass_utils import run_bass_kernel_spmd

    a = {k.removeprefix("L0_"): np.asarray(v) for k, v in inputs.items()}

    def columns(v):
        return v.reshape(-1, P).T

    def by_input(w):
        return w.T.reshape(-1, P, w.shape[0]).transpose(1, 0, 2)

    arrays = {
        "x": a["attn_x"],
        "vectors": np.concatenate([columns(a[k]) for k in (
            "attn_time_mix_k", "attn_time_mix_v", "attn_time_mix_r", "attn_time_decay", "attn_time_first",
            "ffn_w1_s", "ffn_w2_s", "ffn_h1_s", "ffn_h2_s")], axis=1),
        "w_mix": np.stack([by_input(a[f"attn_W_{k}"]) for k in "kvro"], axis=1),
        "w_ffn": np.concatenate([by_input(a[f"ffn_{k}_w"]).reshape(P, -1) for k in (
            "w1", "w2", "h1", "h2", "w3")], axis=1),
        "s3": a["ffn_w3_s"].reshape(1, -1),
    }
    arrays = {f"in_{k}": np.ascontiguousarray(v) for k, v in arrays.items()}
    nc = bacc.Bacc("TRN2", target_bir_lowering=False, num_devices=1)
    args = [nc.dram_tensor(f"in_{k}", arrays[f"in_{k}"].shape, F32, kind="ExternalInput").ap() for k in _ORDER]
    args.append(nc.dram_tensor("out", a["attn_x"].shape, F32, kind="ExternalOutput").ap())
    build(nc, *args)
    r = run_bass_kernel_spmd(nc, [arrays], core_ids=[0])
    return r.results[0]["out"]
```
